# Optimizing a Trainium2 kernel written in Bass

```python
import numpy as np
import jax
import jax.numpy as jnp

def _softmax(x, axis=-1):
    return jax.nn.softmax(x, axis=axis)

def _gelu(x):
    return jax.nn.gelu(x, approximate=True)

def _silu(x):
    return jax.nn.silu(x)

def _sigmoid(x):
    return jax.nn.sigmoid(x)

def _layernorm(x, axis=-1, eps=1e-05):
    m = jnp.mean(x, axis=axis, keepdims=True)
    v = jnp.var(x, axis=axis, keepdims=True)
    return (x - m) / jnp.sqrt(v + eps)

def _scatter_add(tgt, idx, src, axis=0):
    return tgt.at[idx].add(src)

def _segment_sum(src, seg, n):
    return jax.ops.segment_sum(src, seg, n)
kernel_name = 'mk_gps_d1_gnn_r16_bdb38e'

def setup_inputs(seed: int=0):
    np.random.seed(seed)
    _w = jnp.asarray

    def _rec_inputs():
        import jax
        import jax.numpy as jnp
        _gk = jax.random.key(seed)
        x = -0.0003713 + 1 * jax.random.normal(jax.random.fold_in(_gk, 1), (3125, 256), jnp.float32)
        _s = jax.random.randint(jax.random.fold_in(_gk, 2), (50000,), 0, 3125, jnp.int32)
        _d = jax.random.randint(jax.random.fold_in(_gk, 3), (50000,), 0, 3125, jnp.int32)
        _loop = jnp.arange(3125, dtype=jnp.int32)
        src = jnp.concatenate([_s, _d, _loop])
        dst = jnp.concatenate([_d, _s, _loop])
        _o = jnp.argsort(dst, stable=True)
        src = src[_o]
        dst = dst[_o]
        return (x, src, dst)
    x, src, dst = _rec_inputs()

    def _L0_gnn_setup():
        import jax, jax.numpy as jnp
        import numpy as np
        N = 3125
        E = 50000
        D_IN = 256
        D_H = 512
        D_OUT = 256
        key = jax.random.key(seed)
        ks = jax.random.split(key, 12)
        s = lambda d: 1.0 / np.sqrt(d)
        x = jax.random.normal(ks[0], (N, D_IN), dtype=jnp.float32)
        edge_index = jax.random.randint(ks[1], (2, E), 0, N, dtype=jnp.int64)
        W_rel = jax.random.uniform(ks[2], (D_IN, D_H), jnp.float32, -s(D_IN), s(D_IN))
        b_rel = jax.random.uniform(ks[3], (D_H,), jnp.float32, -s(D_IN), s(D_IN))
        W_root = jax.random.uniform(ks[4], (D_IN, D_H), jnp.float32, -s(D_IN), s(D_IN))
        W_ih = jax.random.uniform(ks[5], (4 * D_H, D_H), jnp.float32, -s(D_H), s(D_H))
        W_hh = jax.random.uniform(ks[6], (4 * D_H, D_H), jnp.float32, -s(D_H), s(D_H))
        b_ih = jax.random.uniform(ks[7], (4 * D_H,), jnp.float32, -s(D_H), s(D_H))
        b_hh = jax.random.uniform(ks[8], (4 * D_H,), jnp.float32, -s(D_H), s(D_H))
        W_fc = jax.random.uniform(ks[9], (D_H, D_OUT), jnp.float32, -s(D_H), s(D_H))
        b_fc = jax.random.uniform(ks[10], (D_OUT,), jnp.float32, -s(D_H), s(D_H))
        return {'x': x, 'edge_index': edge_index, 'W_rel': W_rel, 'b_rel': b_rel, 'W_root': W_root, 'W_ih': W_ih, 'W_hh': W_hh, 'b_ih': b_ih, 'b_hh': b_hh, 'W_fc': W_fc, 'b_fc': b_fc}
    _L0_gnn_all = _L0_gnn_setup()
    _L0_gnn_in = {k: v for k, v in _L0_gnn_all.items() if k in ('W_rel', 'b_rel', 'W_root', 'W_ih', 'W_hh', 'b_ih', 'b_hh', 'W_fc', 'b_fc')}
    del _L0_gnn_all

    def _L0_mix_setup():
        import jax, jax.numpy as jnp
        import numpy as np
        HEADS = 8
        EPS = 1e-05

        def _ln(t, w, b, headc):
            m = jnp.mean(t, axis=-1, keepdims=True)
            d = t - m
            std = jnp.sqrt(jnp.sum(d * d, axis=-1, keepdims=True) / (headc - 1))
            return w * (d / (std + EPS)) + b
        key = jax.random.key(seed)
        B, N, C = (32, 256, 256)
        headc = C // HEADS
        x = jax.random.normal(key, (B, N, C), dtype=jnp.float32)
        return {'x': x, 'kln_weight': jnp.ones((HEADS, 1, headc), dtype=jnp.float32), 'kln_bias': jnp.zeros((HEADS, 1, headc), dtype=jnp.float32), 'vln_weight': jnp.ones((HEADS, 1, headc), dtype=jnp.float32), 'vln_bias': jnp.zeros((HEADS, 1, headc), dtype=jnp.float32)}
    _L0_mix_all = _L0_mix_setup()
    _L0_mix_in = {k: v for k, v in _L0_mix_all.items() if k in ('kln_weight', 'kln_bias', 'vln_weight', 'vln_bias')}
    del _L0_mix_all

    def _L0_ffn_setup():
        import jax, jax.numpy as jnp
        import numpy as np
        TOP_K = 2
        LN_EPS = 1e-05
        key = jax.random.key(seed)
        ks = jax.random.split(key, 8)
        B, S, D, E, H = (16, 1024, 256, 8, 1024)
        x = jax.random.normal(ks[0], (B, S, D), dtype=jnp.float32)
        Wr = jax.random.normal(ks[1], (D, E), dtype=jnp.float32) * 0.1
        br = jnp.zeros((E,), dtype=jnp.float32)
        ln_g = jnp.ones((E, D), dtype=jnp.float32)
        ln_b = jnp.zeros((E, D), dtype=jnp.float32)
        W1 = jax.random.normal(ks[2], (E, D, H), dtype=jnp.float32) * (1.0 / np.sqrt(D))
        b1 = jnp.zeros((E, H), dtype=jnp.float32)
        W2 = jax.random.normal(ks[3], (E, H, D), dtype=jnp.float32) * (1.0 / np.sqrt(H))
        b2 = jnp.zeros((E, D), dtype=jnp.float32)
        return {'x': x, 'Wr': Wr, 'br': br, 'ln_g': ln_g, 'ln_b': ln_b, 'W1': W1, 'b1': b1, 'W2': W2, 'b2': b2}
    _L0_ffn_all = _L0_ffn_setup()
    _L0_ffn_in = {k: v for k, v in _L0_ffn_all.items() if k in ('Wr', 'br', 'ln_g', 'ln_b', 'W1', 'b1', 'W2', 'b2')}
    del _L0_ffn_all
    return {'x': x, 'src': src, 'dst': dst, 'L0_gnn_W_rel': _L0_gnn_in['W_rel'], 'L0_gnn_b_rel': _L0_gnn_in['b_rel'], 'L0_gnn_W_root': _L0_gnn_in['W_root'], 'L0_gnn_W_ih': _L0_gnn_in['W_ih'], 'L0_gnn_W_hh': _L0_gnn_in['W_hh'], 'L0_gnn_b_ih': _L0_gnn_in['b_ih'], 'L0_gnn_b_hh': _L0_gnn_in['b_hh'], 'L0_gnn_W_fc': _L0_gnn_in['W_fc'], 'L0_gnn_b_fc': _L0_gnn_in['b_fc'], 'L0_mix_kln_weight': _L0_mix_in['kln_weight'], 'L0_mix_kln_bias': _L0_mix_in['kln_bias'], 'L0_mix_vln_weight': _L0_mix_in['vln_weight'], 'L0_mix_vln_bias': _L0_mix_in['vln_bias'], 'L0_ffn_Wr': _L0_ffn_in['Wr'], 'L0_ffn_br': _L0_ffn_in['br'], 'L0_ffn_ln_g': _L0_ffn_in['ln_g'], 'L0_ffn_ln_b': _L0_ffn_in['ln_b'], 'L0_ffn_W1': _L0_ffn_in['W1'], 'L0_ffn_b1': _L0_ffn_in['b1'], 'L0_ffn_W2': _L0_ffn_in['W2'], 'L0_ffn_b2': _L0_ffn_in['b2']}

def reference(x, src, dst, L0_gnn_W_rel, L0_gnn_b_rel, L0_gnn_W_root, L0_gnn_W_ih, L0_gnn_W_hh, L0_gnn_b_ih, L0_gnn_b_hh, L0_gnn_W_fc, L0_gnn_b_fc, L0_mix_kln_weight, L0_mix_kln_bias, L0_mix_vln_weight, L0_mix_vln_bias, L0_ffn_Wr, L0_ffn_br, L0_ffn_ln_g, L0_ffn_ln_b, L0_ffn_W1, L0_ffn_b1, L0_ffn_W2, L0_ffn_b2):
    import jax
    import jax.numpy as jnp

    def _L0_gnn_ref(x, edge_index, W_rel, b_rel, W_root, W_ih, W_hh, b_ih, b_hh, W_fc, b_fc):
        import jax, jax.numpy as jnp
        import numpy as np
        N = 3125
        E = 50000
        D_IN = 256
        D_H = 512
        D_OUT = 256
        src, dst = (edge_index[0], edge_index[1])
        agg = jax.ops.segment_sum(x[src], dst, num_segments=N)
        h = jax.nn.relu(agg @ W_rel + b_rel + x @ W_root)
        gates = h @ W_ih.T + b_ih + b_hh
        i, f, g, o = jnp.split(gates, 4, axis=-1)
        c = jax.nn.sigmoid(i) * jnp.tanh(g)
        h_lstm = jax.nn.sigmoid(o) * jnp.tanh(c)
        return h_lstm @ W_fc + b_fc

    def _L0_mix_ref(x, kln_weight, kln_bias, vln_weight, vln_bias):
        import jax, jax.numpy as jnp
        import numpy as np
        HEADS = 8
        EPS = 1e-05

        def _ln(t, w, b, headc):
            m = jnp.mean(t, axis=-1, keepdims=True)
            d = t - m
            std = jnp.sqrt(jnp.sum(d * d, axis=-1, keepdims=True) / (headc - 1))
            return w * (d / (std + EPS)) + b
        B, N, C = x.shape
        headc = C // HEADS
        qkv = x.reshape(B, N, HEADS, headc).transpose(0, 2, 1, 3)
        k = _ln(qkv, kln_weight, kln_bias, headc)
        v = _ln(qkv, vln_weight, vln_bias, headc)
        kv = jnp.einsum('bhnd,bhne->bhde', k, v) / N
        out = jnp.einsum('bhnd,bhde->bhne', qkv, kv)
        out = out.transpose(0, 2, 1, 3).reshape(B, N, C)
        return out + x

    def _L0_ffn_ref(x, Wr, br, ln_g, ln_b, W1, b1, W2, b2):
        import jax, jax.numpy as jnp
        import numpy as np
        TOP_K = 2
        LN_EPS = 1e-05
        B, S, D = x.shape
        N = B * S
        xt = x.reshape(N, D)
        logits = xt @ Wr + br
        probs = jax.nn.softmax(logits, axis=-1)
        top_p, top_idx = jax.lax.top_k(probs, TOP_K)
        weights = top_p / top_p.sum(axis=-1, keepdims=True)
        mu = xt.mean(axis=-1, keepdims=True)
        var = ((xt - mu) ** 2).mean(axis=-1, keepdims=True)
        xn = (xt - mu) * jax.lax.rsqrt(var + LN_EPS)
        xe = xn[None, :, :] * ln_g[:, None, :] + ln_b[:, None, :]
        h = jax.nn.gelu(jnp.einsum('end,edh->enh', xe, W1) + b1[:, None, :], approximate=False)
        y = jnp.einsum('enh,ehd->end', h, W2) + b2[:, None, :]
        y_tok = jnp.transpose(y, (1, 0, 2))
        sel = jnp.take_along_axis(y_tok, top_idx[:, :, None], axis=1)
        out = (weights[:, :, None] * sel).sum(axis=1)
        return out.reshape(B, S, D)
    edge_index = jnp.stack([src, dst])
    xn = _layernorm(x, axis=-1)
    x = x + _L0_gnn_ref(xn, edge_index, L0_gnn_W_rel, L0_gnn_b_rel, L0_gnn_W_root, L0_gnn_W_ih, L0_gnn_W_hh, L0_gnn_b_ih, L0_gnn_b_hh, L0_gnn_W_fc, L0_gnn_b_fc) + _L0_mix_ref(xn[None], L0_mix_kln_weight, L0_mix_kln_bias, L0_mix_vln_weight, L0_mix_vln_bias)[0]
    x = x + _L0_ffn_ref(_layernorm(x, axis=-1)[None], L0_ffn_Wr, L0_ffn_br, L0_ffn_ln_g, L0_ffn_ln_b, L0_ffn_W1, L0_ffn_b1, L0_ffn_W2, L0_ffn_b2)[0]
    return x

_drawn_inputs = setup_inputs


def setup_inputs(seed=0):
    import zlib

    import numpy as np

    out = dict(_drawn_inputs(seed))
    spreads = {'L0_mix_kln_weight': (1.0, 0.2),
     'L0_mix_kln_bias': (0.0, 0.351),
     'L0_mix_vln_weight': (1.0, 0.2),
     'L0_mix_vln_bias': (0.0, 0.343),
     'L0_ffn_br': (0.0, 0.1),
     'L0_ffn_ln_g': (1.0, 0.2),
     'L0_ffn_ln_b': (0.0, 0.454),
     'L0_ffn_b1': (0.0, 0.448),
     'L0_ffn_b2': (0.0, 0.314)}
    factors = {'L0_gnn_b_rel': 50.162,
     'L0_gnn_W_root': 4.701,
     'L0_gnn_b_ih': 35.167,
     'L0_gnn_b_hh': 31.27,
     'L0_gnn_b_fc': 4.054}
    for name, (base, spread) in spreads.items():
        noise = np.random.default_rng([zlib.crc32(name.encode()), seed]).standard_normal(out[name].shape)
        drawn = base * np.exp(spread * noise) if base else spread * noise
        out[name] = jnp.asarray(drawn.astype(out[name].dtype))
    for name, factor in factors.items():
        out[name] = (out[name] * factor).astype(out[name].dtype)
    return out
```

```python
import numpy as np
import concourse.bass as bass
from concourse import mybir
from contextlib import ExitStack

F32 = mybir.dt.float32
F32R = mybir.dt.float32r
F16 = mybir.dt.float16
I32 = mybir.dt.int32
U32 = mybir.dt.uint32
ALU = mybir.AluOpType
ACT = mybir.ActivationFunctionType
AX = mybir.AxisListType

NODES, DIM, HID = 3125, 256, 512
EDGES = 103125
EXPERTS, FF = 8, 1024
HEADS, HEADC = 8, 32
P = 128
LN_EPS = 1e-5

TILE = 125
TILES = NODES // TILE
TPG = 2
GROUP = TPG * TILE
FULL_GROUPS = TILES // TPG
GROUPS = FULL_GROUPS + 1
SRC_BLOCKS = -(-NODES // P)
LAST_BLOCK = NODES - (SRC_BLOCKS - 1) * P

WIN = 5
WINDOWS = NODES // WIN
RUN = 256
HALVES = RUN // P
WPI = TPG
ROUNDS = GROUP // (WIN * WPI)
RING = 5
SETS = WINDOWS // TILE
STRIDE = 33
SAMPLES = EDGES // STRIDE
COLS = EDGES // TILE
KEYS = WIN * SRC_BLOCKS

SLOTS = 256
CAP = NODES + SLOTS + 3
ROW = DIM + 4
MAXBLK = 2 * NODES // SLOTS + EXPERTS
KC, HC, MC = DIM // P, HID // P, FF // P
GATES = 3 * HC
RAW = 1024

C_B1, C_LNG, C_LNB = 0, EXPERTS * MC, EXPERTS * MC + EXPERTS * KC
C_BREL = C_LNB + EXPERTS * KC
C_BIH = C_BREL + HC
C_BHH = C_BIH + GATES
C_KW = C_BHH + GATES
C_KB = C_KW + KC

USES = (["xnT0", "xnT1"] + [f"h{m}" for m in range(HC)]
        + [f"{q}{j}" for j in range(2) for q in "igo"] + ["tT"]
        + [f"{q}2" for q in "igo"] + ["logits"] + [f"{q}3" for q in "igo"]
        + ["rank", "fc0", "fc1"])
BANKS = 4


class Steps:

    def __init__(self, eng, sem, base=0, apart=None):
        self.eng, self.sem, self.base, self.n, self.apart = eng, sem, base, 0, apart

    def did(self, ins):
        ins.then_inc(self.sem, 1)
        self.n += 1

    def settle(self):
        self.eng.wait_ge(self.sem, self.base + self.n)
        if self.apart is not None:
            self.eng.sem_inc(self.apart, 1)

    def fill(self, total):
        assert self.n <= total, self.n
        if self.n < total:
            self.eng.sem_inc(self.sem, total - self.n)


class Stage:

    def __init__(self, g, pair, parity, tiles, build_tiles, routes):
        self.g, self.pair, self.parity, self.tiles = g, pair, parity, tiles
        self.build_tiles, self.routes = build_tiles, routes
        self.n = tiles * TILE
        self.even = self.n + self.n % 2


def bank_of(use):
    return USES.index(use) % BANKS


def bank_turn(g, use):
    b, at = bank_of(use), USES.index(use)
    per_stage = len(USES[b::BANKS])
    return g * per_stage + at // BANKS + 1


def each_stage(eng, body):
    body(Stage(0, 0, 0, TPG, TPG, False))
    with eng.Fori(0, (FULL_GROUPS - 2) // 2) as i:
        body(Stage(2 * i + 1, i, 1, TPG, TPG, True))
        body(Stage(2 * i + 2, i + 1, 0, TPG, TPG, True))
    g = FULL_GROUPS - 1
    body(Stage(g, g // 2, g % 2, TPG, TILES - FULL_GROUPS * TPG, True))
    body(Stage(g + 1, (g + 1) // 2, (g + 1) % 2, TILES - FULL_GROUPS * TPG, 0, True))


def pool_stages(eng, body):
    each_stage(eng, body)


DVE_STAGE = 64
POOL_STAGE = 16


def program(nc, x, src, dst, W_rel, b_rel, W_root, W_ih, W_hh, b_ih, b_hh, W_fc, b_fc,
            kln_w, kln_b, vln_w, vln_b, Wr, br, ln_g, ln_b, W1, b1, W2, b2, out):
    samp_d = nc.dram_tensor("samp_d", [SAMPLES], F32).ap()
    ends_d = [nc.dram_tensor(f"{q}_d", [-(-EDGES // RUN) * RUN], I32).ap() for q in ("dst", "src")]
    xn_d = nc.dram_tensor("xn_d", [NODES, DIM], F32).ap()
    rows_d = nc.dram_tensor("rows_d", [EXPERTS * CAP, ROW], F32).ap()
    acc_d = nc.dram_tensor("acc_d", [NODES + SLOTS, DIM], F32).ap()

    with ExitStack() as ctx:
        def sem(name):
            return ctx.enter_context(nc.semaphore(name))

        keep = Memory(nc, ctx)
        keep.ident = keep.sbuf("ident", [P, P], F32)
        keep.colsT = keep.sbuf("colsT", [P, P], F32)
        keep.carry = keep.sbuf("carry", [TILE, EXPERTS], F32)
        keep.raw = keep.sbuf("raw", [P, 2, RAW], F32)
        keep.banks = [ctx.enter_context(nc.psum_tensor(f"bank{i}", [P, 512], F32))
                      for i in range(8)]
        gnn_phase(nc, sem, keep, samp_d, ends_d, xn_d, rows_d, acc_d, x, src, dst, W_rel, b_rel, W_root,
                  W_ih, b_ih, b_hh, W_fc, b_fc, kln_w, kln_b, vln_w, vln_b, Wr, br, ln_g, ln_b,
                  b1)
        moe_phase(nc, sem, keep, rows_d, acc_d, W1, W2, b2, out)


class Memory:

    def __init__(self, nc, stack):
        self.nc, self.stack = nc, stack

    def sbuf(self, name, shape, dt):
        return self.stack.enter_context(self.nc.sbuf_tensor(name, shape, dt))


def mm3(nc, out, lhs, rhs, start, stop):
    (lh, ll), (rh, rl) = lhs, rhs
    nc.tensor.matmul(out, lh, rh, start=start, stop=False)
    nc.tensor.matmul(out, lh, rl, start=False, stop=False)
    return nc.tensor.matmul(out, ll, rh, start=False, stop=stop)


def gnn_phase(nc, sem, keep, samp_d, ends_d, xn_d, rows_d, acc_d, x, src, dst, W_rel, b_rel, W_root,
              W_ih, b_ih, b_hh, W_fc, b_fc, kln_w, kln_b, vln_w, vln_b, Wr, br, ln_g, ln_b, b1):
    ident, colsT, carry, raw = keep.ident, keep.colsT, keep.carry, keep.raw
    gen, ps_cnt, ps_agg = keep.banks[0:4], keep.banks[4:6], keep.banks[6:8]

    with ExitStack() as ctx:
        m = Memory(nc, ctx)
        ones = m.sbuf("ones", [P, P], F32)
        tri = m.sbuf("tri", [TILE, TILE], F32)
        iota8 = m.sbuf("iota8", [TILE, EXPERTS], F32)
        iota_rep = m.sbuf("iota_rep", [P, P, WPI * HALVES], F16)
        ids = m.sbuf("ids", [TILE, TILES], F32)
        half_pow = m.sbuf("half_pow", [P, 2, 5 * HEADS], F32)
        zeros = m.sbuf("zeros", [P, DIM], F32)
        xn16 = m.sbuf("xn16", [P, 2, SRC_BLOCKS, DIM], F16)
        w_rel = [m.sbuf(f"w_rel{q}", [P, KC, HID], F32R) for q in "hl"]
        w_root = [m.sbuf(f"w_root{q}", [P, KC, HID], F32R) for q in "hl"]
        w_fc = [m.sbuf(f"w_fc{q}", [P, HC, DIM], F32R) for q in "hl"]
        w_ih = [m.sbuf(f"w_ih{q}", [P, HC, GATES * P], F32R) for q in "hl"]
        kv = [m.sbuf(f"kv{q}", [P, KC, P], F32R) for q in "hl"]
        w_r = m.sbuf("w_r", [P, KC, EXPERTS], F32)
        br_b = m.sbuf("br_b", [TILE, EXPERTS], F32)
        bfc_b = m.sbuf("bfc_b", [TILE, DIM], F32)
        bg = m.sbuf("bg", [P, GATES], F32)
        counts = m.sbuf("counts", [P, 2, SRC_BLOCKS, GROUP], F16)
        a_tab = m.sbuf("a_tab", [P, WINDOWS * HALVES], F16)
        k_tab = m.sbuf("k_tab", [P, WINDOWS * HALVES], F16)
        oh_a = m.sbuf("oh_a", [P, RING, P * WPI * HALVES], F16)
        oh_k = m.sbuf("oh_k", [P, RING, KEYS * WPI * HALVES], F16)

        with ExitStack() as early:
            e = Memory(nc, early)
            xs = e.sbuf("xs", [P, SRC_BLOCKS, DIM], F32)
            dst_raw = e.sbuf("dst_raw", [TILE, COLS], I32)
            samp = e.sbuf("samp", [TILE, SAMPLES // TILE], F32)
            samp_b = e.sbuf("samp_b", [P, SAMPLES], F32)
            e_dst = e.sbuf("e_dst", [TILE, SETS, RUN], I32)
            e_src_all = e.sbuf("e_src", [P, SETS, RUN], I32)
            e_src = e_src_all[0:TILE, :, :]
            e_blk = samp_b[0:TILE, 0:SETS * RUN].bitcast(I32)
            e_ok = samp_b[0:TILE, SETS * RUN:2 * SETS * RUN]
            thr = e.sbuf("thr", [TILE, SETS], F32)
            cnt = e.sbuf("cnt", [TILE, 2 * SETS], F32)
            start = e.sbuf("start", [TILE, SETS], U32)
            n_ok = e.sbuf("n_ok", [TILE, 1], F32)
            bn = e.sbuf("bn", [P, 5, 6], F32)
            mv = e.sbuf("mv", [P, SRC_BLOCKS, 2], F32)
            rstd = e.sbuf("rstd", [P, 2, SRC_BLOCKS], F32)
            head = e.sbuf("head", [P, 3, 5 * HEADS], F32)
            prow = e.sbuf("prow", [P, P], F32)
            mask = e.sbuf("mask", [P, P], F32)
            wv_b = e.sbuf("wv_b", [P, DIM], F32)
            bv_b = e.sbuf("bv_b", [P, DIM], F32)
            kvt = e_src_all[:, 0:2, :].rearrange("p a (b c) -> p (a b) c", c=P).bitcast(F32)
            sd = e.sbuf("sd", [P, 1], F32)
            squares = samp_b[:, 0:5 * DIM].rearrange("p (b f) -> p b f", f=DIM)
        agg = [m.sbuf(f"agg{q}", [P, KC, GROUP], F32R) for q in "hl"]
        xnT = [m.sbuf(f"xnT{q}", [P, KC, GROUP], F32R) for q in "hl"]
        h32 = m.sbuf("h32", [P, 2, GROUP], F32)
        hT = [m.sbuf(f"hT{q}", [P, HC, GROUP], F32R) for q in "hl"]
        gate = m.sbuf("gate", [P, 2, 3, GROUP], F32)
        cell = m.sbuf("cell", [P, 2, 2, GROUP], F32)
        out32 = h32
        outT = [m.sbuf(f"outT{q}", [P, HC, GROUP], F32R) for q in "hl"]
        x_row = m.sbuf("x_row", [TILE, 2, TPG, DIM], F32)
        xn_row = m.sbuf("xn_row", [TILE, 2, TPG, DIM], F32)
        x2 = m.sbuf("x2", [TILE, 2, TPG, DIM], F32)
        t_row = m.sbuf("t_row", [TILE, TPG, DIM], F32)
        rows = m.sbuf("rows", [TILE, TPG, ROW], F32)
        tT = m.sbuf("tT", [P, TPG, KC, TILE], F32)
        bn2 = m.sbuf("bn2", [TILE, TPG, 6], F32)
        mv2 = m.sbuf("mv2", [TILE, TPG, 2], F32)
        rs2 = m.sbuf("rs2", [TILE, 2, TPG], F32)
        lg = m.sbuf("lg", [TILE, TPG, EXPERTS], F32)
        m8 = m.sbuf("m8", [TILE, TPG, 8], F32)
        i8 = m.sbuf("i8", [TILE, TPG, 8], U32)
        i8f = m.sbuf("i8f", [TILE, TPG, 2], F32)
        d12 = m.sbuf("d12", [TILE, TPG, 1], F32)
        sel = m.sbuf("sel", [TILE, 3, TPG, EXPERTS], F32)
        pos = m.sbuf("pos", [TILE, TPG, EXPERTS], F32)
        posx = m.sbuf("posx", [TILE, 2, TPG, EXPERTS], F32)
        posf = m.sbuf("posf", [TILE, TPG, 2], F32)
        posu = m.sbuf("posu", [TILE, TPG, 2], U32)

        ld_dst, ld_par, ld_small, ld_sampb, st_samp = (
            sem(n) for n in ("ld_dst", "ld_par", "ld_small", "ld_sampb", "st_samp"))
        ld_x = [sem(f"ld_x{c}") for c in range(5)]
        ld_raw = [sem(f"ld_raw{c}") for c in range(2)]
        ld_whi, ld_edges, st_xn, st_zero = (
            sem(n) for n in ("ld_whi", "ld_edges", "st_xn", "st_zero"))
        st_ends = sem("st_ends")
        pad_ready, const_ready, samp_ready, start_ready = (
            sem(n) for n in ("pad_ready", "const_ready", "samp_ready", "start_ready"))
        mv_ready, rstd_ready, xn_ready, xnh_ready, xnl_ready = (
            sem(n) for n in ("mv_ready", "rstd_ready", "xn_ready", "xnh_ready", "xnl_ready"))
        head_sum, head_dev, head_sq, head_ss, head_std, head_inv, z_ready = (
            sem(n) for n in ("head_sum", "head_dev", "head_sq", "head_ss", "head_std",
                             "head_inv", "z_ready"))
        keys_ready, tab_ready, wlo_ready, raw_used, wih_hi, cols_ready, kv_ready = (
            sem(n) for n in ("keys_ready", "tab_ready", "wlo_ready", "raw_used", "wih_hi",
                             "cols_ready", "kv_ready"))
        pro_ready = [sem(f"pro_ready{b}") for b in range(BANKS)]
        pro_free = [sem(f"pro_free{b}") for b in range(BANKS)]
        oh_ready, cnt_ready, cnt_taken, agg_ready, agg_hi, agg_lo = (
            sem(n) for n in ("oh_ready", "cnt_ready", "cnt_taken", "agg_ready",
                             "agg_hi", "agg_lo"))
        gready = [sem(f"gready{b}") for b in range(BANKS)]
        gfree = [sem(f"gfree{b}") for b in range(BANKS)]
        ld_rows = [sem(f"ld_rows{b}") for b in range(2)]
        st_x2 = [sem(f"st_x2{b}") for b in range(2)]
        xn_hi, h_hi, h_lo, c_ready, tc_ready, hl_ready, hl_hi, hl_lo, x2_ready = (
            sem(n) for n in ("xn_hi", "h_hi", "h_lo", "c_ready", "tc_ready", "hl_ready",
                             "hl_hi", "hl_lo", "x2_ready"))
        var_ready, rs_ready, t_ready, d_ready, w_ready, sel_ready, pos_ready, scattered = (
            sem(n) for n in ("var_ready", "rs_ready", "t_ready", "d_ready", "w_ready",
                             "sel_ready", "pos_ready", "scattered"))
        dve_step, act_step, pool_step = sem("dve_step"), sem("act_step"), sem("pool_step")
        dve_apart, pool_apart = sem("dve_apart"), sem("pool_apart")
        end_ready, end_free = sem("end_ready"), sem("end_free")

        PRO = (["cols"] + [f"{q}{k}" for k in range(SETS) for q in "ak"]
               + ["G0", "G1", "S"] + [f"w{c}" for c in range(GATES)])

        def pro(use):
            at = PRO.index(use)
            return at % BANKS, at // BANKS + 1

        ENDS = ["tT", "logits", "rank"]

        class Use:

            def __init__(self, s, name):
                if isinstance(s.g, int) and s.g == GROUPS:
                    n = ENDS.index(name)
                    self.bank, self.ready, self.free = ps_agg[n % 2], end_ready, end_free
                    self.turn, self.before = n + 1, n
                else:
                    b = bank_of(name)
                    self.bank, self.ready, self.free = gen[b], gready[b], gfree[b]
                    self.turn = bank_turn(s.g, name)
                    self.before = bank_turn(s.g, name) - 1 if isinstance(s.g, int) else \
                        bank_turn(s.g, name) + (-1)

        block = ctx.enter_context(nc.Block())
        dst_v = dst.rearrange("(p c) -> p c", p=TILE)

        def xs_chunk(c):
            return xs[:, 5 * c:5 * c + 5, :]

        @block.sync
        def _(sp):
            sp.dma_start(dst_raw[:, :], dst_v).then_inc(ld_dst, 16)
            for to, of in zip(ends_d, (dst, src)):
                sp.dma_start(to[0:EDGES].rearrange("(p c) -> p c", p=TILE),
                             of.rearrange("(p c) -> p c", p=TILE)).then_inc(st_ends, 16)
            for c in range(5):
                if c < 4:
                    sp.dma_start(xs_chunk(c), x[640 * c:640 * c + 640, :].rearrange(
                        "(b p) f -> p b f", p=P)).then_inc(ld_x[c], 16)
                else:
                    sp.wait_ge(pad_ready, 1)
                    sp.dma_start(xs[:, 20:24, :], x[2560:3072, :].rearrange(
                        "(b p) f -> p b f", p=P)).then_inc(ld_x[c], 16)
                    sp.dma_start(xs[0:LAST_BLOCK, 24, :], x[3072:NODES, :]).then_inc(ld_x[c], 16)
                if c == 0:
                    sp.wait_ge(samp_ready, 1)
                    sp.dma_start(samp_d.rearrange("(p c) -> p c", p=TILE), samp[:, :]).then_inc(
                        st_samp, 16)
                    sp.wait_ge(st_samp, 16)
                    sp.dma_start(samp_b[0:TILE, :], samp_d.unsqueeze(0).broadcast_to(
                        [TILE, SAMPLES])).then_inc(ld_sampb, 16)
            for at, n, a in ((C_B1, 64, b1.rearrange("e (m c) -> (e m) c", c=P)),
                             (C_LNG, 16, ln_g.rearrange("e (k c) -> (e k) c", c=P)),
                             (C_LNB, 16, ln_b.rearrange("e (k c) -> (e k) c", c=P)),
                             (C_BREL, HC, b_rel.rearrange("(m c) -> m c", c=P)),
                             (C_BIH, HC, b_ih[0:HID].rearrange("(m c) -> m c", c=P)),
                             (C_BIH + HC, 2 * HC, b_ih[2 * HID:4 * HID].rearrange(
                                 "(m c) -> m c", c=P)),
                             (C_BHH, HC, b_hh[0:HID].rearrange("(m c) -> m c", c=P)),
                             (C_BHH + HC, 2 * HC, b_hh[2 * HID:4 * HID].rearrange(
                                 "(m c) -> m c", c=P)),
                             (C_KW, KC, kln_w.rearrange("(k h) o c -> k (h o c)", k=KC)),
                             (C_KB, KC, kln_b.rearrange("(k h) o c -> k (h o c)", k=KC))):
                sp.dma_start(prow[at:at + n, :], a).then_inc(ld_par, 16)
            sp.dma_start(wv_b[:, :], vln_w.rearrange("h o c -> o (h c)").broadcast_to(
                [P, DIM])).then_inc(ld_small, 16)
            sp.dma_start(bv_b[:, :], vln_b.rearrange("h o c -> o (h c)").broadcast_to(
                [P, DIM])).then_inc(ld_small, 16)
            sp.dma_start(bfc_b[:, :], b_fc.unsqueeze(0).broadcast_to([TILE, DIM])).then_inc(
                ld_small, 16)
            sp.dma_start(br_b[:, :], br.unsqueeze(0).broadcast_to([TILE, EXPERTS])).then_inc(
                ld_small, 16)
            sp.dma_start(w_r[:, :, :], Wr.rearrange("(k p) e -> p k e", p=P)).then_inc(
                ld_small, 16)
            for c in range(5):
                sp.wait_ge(xn_ready, c + 1)
                if c < 4:
                    sp.dma_start(xn_d[640 * c:640 * c + 640, :].rearrange(
                        "(b p) f -> p b f", p=P), xs_chunk(c)).then_inc(st_xn, 16)
                else:
                    sp.dma_start(xn_d[2560:3072, :].rearrange("(b p) f -> p b f", p=P),
                                 xs[:, 20:24, :]).then_inc(st_xn, 16)
                    sp.dma_start(xn_d[3072:NODES, :], xs[0:LAST_BLOCK, 24, :]).then_inc(
                        st_xn, 16)
            items = [W_rel.rearrange("(k p) n -> p k n", p=P),
                     W_root.rearrange("(k p) n -> p k n", p=P),
                     W_fc.rearrange("(k p) n -> p k n", p=P)]
            for c in range(0, GATES, 2):
                row = HID * (0, 2, 3)[c // HC] + P * (c % HC)
                items.append(W_ih[row:row + 2 * P, :].rearrange("(c p) n -> p c n", p=P))
            for j, item in enumerate(items):
                if 2 <= j < 5:
                    sp.wait_ge(wlo_ready, j - 1)
                elif j >= 5:
                    sp.wait_ge(raw_used, j - 4)
                k = item.shape[1]
                sp.dma_start(raw[:, j % 2, :].rearrange("p (k n) -> p k n", k=k), item).then_inc(
                    ld_raw[j % 2], 16)
            sp.wait_ge(const_ready, 1)
            for h in range(SLOTS // P):
                sp.dma_start(acc_d[NODES + h * P:NODES + (h + 1) * P, :], zeros[:, :]).then_inc(
                    st_zero, 16)

            def load_rows(g, parity, tiles):
                n = tiles * TILE
                sp.dma_start(xn_row[:, parity, 0:tiles, :], xn_d[bass.ds(g * GROUP, n), :]
                             .rearrange("(u p) f -> p u f", p=TILE)).then_inc(ld_rows[parity], 16)
                sp.dma_start(x_row[:, parity, 0:tiles, :], x[bass.ds(g * GROUP, n), :]
                             .rearrange("(u p) f -> p u f", p=TILE)).then_inc(ld_rows[parity], 16)

            sp.wait_ge(st_xn, 96)
            sp.wait_ge(kv_ready, 1)
            load_rows(0, 0, TPG)

            def stage(s):
                if s.build_tiles:
                    if not (isinstance(s.g, int) and s.g == 0):
                        sp.wait_ge(x2_ready, s.g)
                    load_rows(s.g + 1, 1 - s.parity, s.build_tiles)
                sp.wait_ge(x2_ready, s.g + 1)
                sp.dma_start(acc_d[bass.ds(s.g * GROUP, s.n), :].rearrange(
                    "(u p) f -> p u f", p=TILE), x2[:, s.parity, 0:s.tiles, :]).then_inc(
                        st_x2[s.parity], 16)

            each_stage(sp, stage)
            sp.wait_ge(st_zero, 16 * (SLOTS // P))
            sp.wait_ge(st_x2[0], 16 * ((GROUPS + 1) // 2))
            sp.wait_ge(st_x2[1], 16 * (GROUPS // 2))

        @block.gpsimd
        def _(pool):
            g_ = nc.gpsimd
            me = Steps(pool, pool_step)
            g_.memset(xs[:, SRC_BLOCKS - 1, :], 0.0).then_inc(pad_ready, 1)
            g_.memset(half_pow[:, 0, :], -0.5)
            g_.memset(half_pow[:, 1, :], 0.5)
            g_.iota(thr[:, :], pattern=[[WIN * TILE, SETS]], base=0, channel_multiplier=WIN,
                    allow_small_or_imprecise_dtypes=True)
            me.did(g_.memset(ident[:, :], 0.0))
            me.settle()
            g_.affine_select(out=ident[:, :], in_=ident[:, :], compare_op=ALU.not_equal, fill=1.0,
                             base=0, pattern=[[-1, P]], channel_multiplier=1)
            g_.memset(ones[:, :], 1.0)
            g_.memset(zeros[:, :], 0.0)
            g_.iota(iota8[:, :], pattern=[[1, EXPERTS]], base=0, channel_multiplier=0,
                    allow_small_or_imprecise_dtypes=True)
            g_.iota(carry[:, :], pattern=[[CAP, EXPERTS]], base=0, channel_multiplier=0,
                    allow_small_or_imprecise_dtypes=True)
            g_.iota(ids[:, :], pattern=[[TILE, TILES]], base=0, channel_multiplier=1,
                    allow_small_or_imprecise_dtypes=True)
            g_.iota(iota_rep[:, :, :], pattern=[[1, P], [0, WPI * HALVES]], base=0,
                    channel_multiplier=0, allow_small_or_imprecise_dtypes=True)
            me.did(g_.memset(mask[:, :], 0.0))
            me.settle()
            for q in range(P // HEADC):
                me.did(g_.memset(mask[HEADC * q:HEADC * q + HEADC,
                                      HEADC * q:HEADC * q + HEADC], 1.0 / NODES))
                me.settle()
            me.did(g_.memset(tri[:, :], 1.0))
            me.settle()
            g_.affine_select(out=tri[:, :], in_=tri[:, :], compare_op=ALU.is_gt, fill=0.0,
                             base=0, pattern=[[1, TILE]], channel_multiplier=-1).then_inc(
                                 const_ready, 1)
            for hi, w in ((w_rel[0], W_rel), (w_root[0], W_root), (w_fc[0], W_fc)):
                pool.dma_start(hi[:, :, :], w.rearrange("(k p) n -> p k n", p=P)).then_inc(
                    ld_whi, 16)
            for c in range(5):
                pool.wait_ge(mv_ready, c + 1)
                r = rstd[:, 0, 5 * c:5 * c + 5]
                q = rstd[:, 1, 5 * c:5 * c + 5]
                me.did(g_.tensor_scalar(q, mv[:, 5 * c:5 * c + 5, 1], LN_EPS, None, ALU.add))
                me.settle()
                me.did(g_.tensor_tensor(r, q, half_pow[:, 0, 0:5], ALU.pow))
                me.settle()
                me.did(g_.tensor_tensor(q, mv[:, 5 * c:5 * c + 5, 0], r, ALU.mult))
                me.settle()
                g_.tensor_scalar(q, q, -1.0, None, ALU.mult).then_inc(rstd_ready, 1)
            pool.wait_ge(start_ready, 1)
            pool.wait_ge(st_ends, 32)
            for k in range(SETS):
                for to, of in zip((e_dst, e_src), ends_d):
                    table = of.rearrange("(a b) -> a b", b=RUN)
                    pool.indirect_dma_start(
                        out=to[:, k, :], out_offset=None, in_=table,
                        in_offset=bass.IndirectOffsetOnAxis(ap=start[:, k:k + 1], axis=1)
                    ).then_inc(ld_edges, 16)
            for c in range(5):
                pool.wait_ge(head_sum, c + 1)
                pool.wait_ge(st_xn, 96)
                v = xs_chunk(c).rearrange("p b (h c) -> p (b h) c", c=HEADC)
                mean = head[:, 0, :].unsqueeze(2).broadcast_to([P, 5 * HEADS, HEADC])
                g_.tensor_tensor(v, v, mean, ALU.subtract).then_inc(head_dev, 1)
                pool.wait_ge(head_ss, c + 1)
                g_.tensor_tensor(head[:, 1, :], head[:, 1, :], half_pow[:, 1, 0:5 * HEADS],
                                 ALU.pow).then_inc(head_std, 1)
                pool.wait_ge(head_inv, c + 1)
                inv = head[:, 2, :].unsqueeze(2).broadcast_to([P, 5 * HEADS, HEADC])
                g_.tensor_tensor(v, v, inv, ALU.mult).then_inc(z_ready, 1)
            pool.wait_ge(ld_whi, 48)
            for j, (hi, lo) in enumerate((w_rel, w_root, w_fc)):
                pool.wait_ge(ld_raw[j % 2], 16 * (j // 2 + 1))
                g_.tensor_tensor(lo[:, :, :].rearrange("p k n -> p (k n)"), raw[:, j % 2, :],
                                 hi[:, :, :].rearrange("p k n -> p (k n)"),
                                 ALU.subtract).then_inc(wlo_ready, 1)

            def route(s, r, parity, tiles):
                st = Steps(pool, pool_step, r * POOL_STAGE + POOL_START, pool_apart)
                for turn in range(2):
                    pool.wait_ge(var_ready, 2 * r + turn + 1)
                    pool.sem_inc(pool_apart, 1)
                    st.did(g_.tensor_scalar(rs2[:, 0, 0:tiles], mv2[:, 0:tiles, 1], LN_EPS, None,
                                            ALU.add))
                    st.settle()
                    g_.tensor_tensor(rs2[:, 1, 0:tiles], rs2[:, 0, 0:tiles],
                                     half_pow[0:TILE, 0, 0:tiles], ALU.pow).then_inc(rs_ready, 1)
                st.fill(POOL_STAGE)
                pool.wait_ge(w_ready, r + 1)
                pool.wait_ge(pos_ready, r + 1)
                pool.sem_inc(pool_apart, 1)
                for u in range(tiles):
                    for c in range(2):
                        pool.indirect_dma_start(
                            out=rows_d, out_offset=bass.IndirectOffsetOnAxis(
                                ap=posu[:, u, c:c + 1], axis=0),
                            in_=rows[:, u, :], in_offset=None).then_inc(scattered, 16)

            POOL_START = 32
            me.fill(POOL_START)

            def stage(s):
                if s.routes:
                    route(s, s.g + (-1), 1 - s.parity, TPG)

            pool_stages(pool, stage)
            route(None, GROUPS - 1, 0, TILES - FULL_GROUPS * TPG)
            pool.wait_ge(scattered, 32 * TILES)

        @block.scalar
        def _(act):
            a_ = nc.scalar
            me = Steps(act, act_step)
            b, turn = pro("cols")
            act.wait_ge(pro_ready[b], turn)
            a_.activation(colsT[:, :], gen[b][:, 0:P], ACT.Copy).then_inc(pro_free[b], 1)
            for c in range(5):
                act.wait_ge(ld_x[c], 16 if c < 4 else 32)
                act.wait_ge(rstd_ready, c + 1)
                for t in range(5 * c, 5 * c + 5):
                    ins = a_.activation(xs[:, t, :], xs[:, t, :], ACT.Identity,
                                        bias=rstd[:, 1, t:t + 1], scale=rstd[:, 0, t:t + 1])
                ins.then_inc(xn_ready, 1)
                act.wait_ge(xn_ready, c + 1)
                a_.activation(xn16[:, 0, 5 * c:5 * c + 5, :], xs_chunk(c), ACT.Copy).then_inc(
                    xnh_ready, 1)
            for k in range(SETS):
                for q, tab in (("a", a_tab), ("k", k_tab)):
                    b, turn = pro(f"{q}{k}")
                    act.wait_ge(pro_ready[b], turn)
                    to = tab[:, k * HALVES * TILE:(k + 1) * HALVES * TILE]
                    a_.activation(to.rearrange("p (w h) -> p h w", h=HALVES),
                                  gen[b][:, 0:HALVES * TILE].rearrange("p (h w) -> p h w",
                                                                       h=HALVES),
                                  ACT.Copy).then_inc(pro_free[b], 1)
            for c in range(5):
                act.wait_ge(head_dev, c + 1)
                act.wait_ge(keys_ready, 1)
                if c:
                    act.wait_ge(head_ss, c)
                a_.activation(squares, xs_chunk(c), ACT.Square).then_inc(head_sq, 1)

            def take_counts(g, tiles):
                parity = g[1]
                def one(it, r):
                    n = ROUNDS * g[0] + it
                    act.wait_ge(cnt_ready, n + (1 + RING))
                    w = tiles * WIN
                    to = counts[:, parity, :, bass.ds(it * w, w)].rearrange(
                        "p b (u j) -> p b u j", j=WIN)
                    of = ps_cnt[r % 2][:, 0:tiles * KEYS].rearrange(
                        "p (u b j) -> p b u j", u=tiles, j=WIN)
                    a_.activation(to, of, ACT.Copy).then_inc(cnt_taken, 1)
                with act.Fori(0, ROUNDS // RING) as i:
                    for r in range(RING):
                        one(i * RING + r, r)

            take_counts((0, 0), TPG)
            for c in range(GATES):
                b, turn = pro(f"w{c}")
                act.wait_ge(pro_ready[b], turn)
                a_.activation(w_ih[0][:, :, c * P:(c + 1) * P],
                              gen[b][:, :].rearrange("p (k n) -> p k n", k=HC),
                              ACT.Copy).then_inc(wih_hi, 1)

            def stage(s):
                n = s.n
                for k in range(KC):
                    u = Use(s, f"xnT{k}")
                    act.wait_ge(u.ready, u.turn)
                    a_.activation(xnT[0][:, k, 0:n], u.bank[:, 0:n], ACT.Copy).then_inc(xn_hi, 1)
                if s.build_tiles:
                    take_counts((s.g + 1, 1 - s.parity), s.build_tiles)
                act.wait_ge(agg_ready, s.g + 1)
                a_.activation(agg[0][:, 0, 0:n], ps_agg[0][:, 0:n], ACT.Copy)
                a_.activation(agg[0][:, 1, 0:n], ps_agg[1][:, 0:n], ACT.Copy).then_inc(agg_hi, 1)
                for i in range(HC):
                    u = Use(s, f"h{i}")
                    act.wait_ge(u.ready, u.turn)
                    if i >= 2:
                        act.wait_ge(h_lo, s.g * HC + i - 1)
                    a_.activation(h32[:, i % 2, 0:n], u.bank[:, 0:n], ACT.Relu,
                                  bias=colsT[:, C_BREL + i:C_BREL + i + 1]).then_inc(u.free, 1)
                    act.wait_ge(u.free, u.turn)
                    a_.activation(hT[0][:, i, 0:n], h32[:, i % 2, 0:n], ACT.Copy).then_inc(
                        h_hi, 1)

                def gates(j):
                    for q, f in enumerate((ACT.Sigmoid, ACT.Tanh, ACT.Sigmoid)):
                        u = Use(s, f"{'igo'[q]}{j}")
                        act.wait_ge(u.ready, u.turn)
                        a_.activation(gate[:, j % 2, q, 0:n], u.bank[:, 0:n], f,
                                      bias=bg[:, q * HC + j:q * HC + j + 1]).then_inc(u.free, 1)
                    act.wait_ge(c_ready, s.g * HC + j + 1)
                    a_.activation(cell[:, j % 2, 1, 0:n], cell[:, j % 2, 0, 0:n],
                                  ACT.Tanh).then_inc(tc_ready, 1)
                    act.wait_ge(hl_ready, s.g * HC + j + 1)
                    a_.activation(outT[0][:, j, 0:n], out32[:, j % 2, 0:n], ACT.Copy).then_inc(
                        hl_hi, 1)

                gates(0)
                gates(1)
                if s.routes:
                    take_tT(s, TPG)
                gates(2)
                if s.routes:
                    weights(s.g + (-1), TPG)
                gates(3)

            def take_tT(s, tiles):
                u = Use(s, "tT")
                act.wait_ge(u.ready, u.turn)
                a_.activation(tT[:, 0:tiles, :, :].rearrange("p u k n -> p (u k n)"),
                              u.bank[:, 0:tiles * KC * TILE], ACT.Copy).then_inc(u.free, 1)

            def weights(r, tiles):
                act.wait_ge(d_ready, r + 1)
                a_.activation(rows[:, 0:tiles, DIM + 2:DIM + 3], d12[:, 0:tiles, :], ACT.Sigmoid)
                a_.activation(rows[:, 0:tiles, DIM + 3:DIM + 4], d12[:, 0:tiles, :], ACT.Sigmoid,
                              scale=-1.0).then_inc(w_ready, 1)

            each_stage(act, stage)
            end = Stage(GROUPS, 0, 0, TILES - FULL_GROUPS * TPG, 0, True)
            take_tT(end, end.tiles)
            weights(GROUPS - 1, end.tiles)

        @block.tensor
        def _(pe):
            t_ = nc.tensor
            pe.sem_inc(cnt_taken, 2)
            pe.sem_inc(cnt_ready, RING)
            pe.wait_ge(const_ready, 1)
            pe.wait_ge(ld_par, 160)
            b, _ = pro("cols")
            t_.transpose(gen[b][:, 0:P], prow[:, :], ident[:, :]).then_inc(pro_ready[b], 1)
            pe.wait_ge(keys_ready, 1)
            for k in range(SETS):
                for q, tab in (("a", e_src), ("k", e_dst)):
                    b, turn = pro(f"{q}{k}")
                    if turn > 1:
                        pe.wait_ge(pro_free[b], turn - 1)
                    for h in range(HALVES):
                        ins = t_.transpose(gen[b][:, h * TILE:(h + 1) * TILE],
                                           tab[:, k, h * P:(h + 1) * P].bitcast(F32),
                                           ident[0:TILE, 0:TILE])
                    ins.then_inc(pro_ready[b], 1)

            def build(g, it, r, tiles):
                n = ROUNDS * g + it
                pe.wait_ge(oh_ready, n + 1)
                pe.wait_ge(cnt_taken, n + (2 if r == 0 else 1))
                T = tiles * HALVES
                a = oh_a[:, r, 0:P * T].rearrange("p (a t) -> p a t", t=T)
                k = oh_k[:, r, 0:KEYS * T].rearrange("p (k t) -> p k t", t=T)
                for u in range(tiles):
                    for h in range(HALVES):
                        ins = t_.matmul(ps_cnt[r % 2][:, u * KEYS:(u + 1) * KEYS],
                                        a[:, :, u * HALVES + h], k[:, :, u * HALVES + h],
                                        start=(h == 0), stop=(h == HALVES - 1))
                        if u == tiles - 1 and h == 0 and False:
                            pass
                ins.then_inc(cnt_ready, 1)

            def aggregate(s, it, first, last):
                for k in range(KC):
                    for q in range(2):
                        ins = t_.matmul(ps_agg[k][:, 0:s.n],
                                        xn16[:, q, it, k * P:(k + 1) * P],
                                        counts[:, s.parity, it, 0:s.n],
                                        start=first and q == 0, stop=last and q == 1)
                if last:
                    ins.then_inc(agg_ready, 1)

            def build_first(i):
                for r in range(RING):
                    build(0, i * RING + r, r, TPG)

            with pe.Fori(0, ROUNDS // RING) as i:
                build_first(i)

            bg0, bg1, bs = pro("G0")[0], pro("G1")[0], pro("S")[0]
            for use in ("G0", "G1", "S"):
                b, turn = pro(use)
                pe.wait_ge(pro_free[b], turn - 1)
            for c in range(5):
                pe.wait_ge(z_ready, c + 1)
                for t in range(5 * c, 5 * c + 5):
                    first, last = t == 0, t == SRC_BLOCKS - 1
                    for k, bb in enumerate((bg0, bg1)):
                        z = xs[:, t, k * P:(k + 1) * P]
                        ins = t_.matmul(gen[bb][:, 0:P], z, z, start=first, stop=last)
                        if last:
                            ins.then_inc(pro_ready[bb], 1)
                    ins = t_.matmul(gen[bs][:, 0:DIM], ones[:, :], xs[:, t, :], start=first,
                                    stop=last)
                    if last:
                        ins.then_inc(pro_ready[bs], 1)
            for c in range(GATES):
                j = 3 + c // 2
                pe.wait_ge(ld_raw[j % 2], 16 * (j // 2 + 1))
                b, turn = pro(f"w{c}")
                pe.wait_ge(pro_free[b], turn - 1)
                for k in range(HC):
                    at = (c % 2) * HID + k * P
                    ins = t_.transpose(gen[b][:, k * P:(k + 1) * P], raw[:, j % 2, at:at + P],
                                       ident[:, :])
                ins.then_inc(pro_ready[b], 1)
                if c % 2 == 1:
                    pe.wait_ge(pro_ready[b], turn)
                    pe.sem_inc(raw_used, 1)
            for b in range(BANKS):
                pe.wait_ge(pro_free[b], len(PRO[b::BANKS]))
            pe.wait_ge(wlo_ready, 3)
            pe.wait_ge(ld_whi, 48)
            pe.wait_ge(xnl_ready, 5)
            pe.wait_ge(ld_small, 80)
            pe.wait_ge(kv_ready, 1)

            def hl(pair, *idx):
                return tuple(t[idx] for t in pair)

            def stage(s):
                n, ne = s.n, s.even
                pe.wait_ge(ld_rows[s.parity], (s.pair + 1) * 32)
                for k in range(KC):
                    u = Use(s, f"xnT{k}")
                    if not (isinstance(u.before, int) and u.before == 0):
                        pe.wait_ge(u.free, u.before)
                    for v in range(s.tiles):
                        ins = t_.transpose(u.bank[:, v * TILE:(v + 1) * TILE],
                                           xn_row[:, s.parity, v, k * P:(k + 1) * P],
                                           ident[0:TILE, 0:TILE])
                    ins.then_inc(u.ready, 1)
                pe.wait_ge(cnt_taken, (s.g + 1) * ROUNDS + 2)
                if not (isinstance(s.g, int) and s.g == 0):
                    pe.wait_ge(agg_lo, s.g)

                def five(i, first, last):
                    for r in range(RING):
                        it = i * RING + r
                        if s.build_tiles:
                            build(s.g + 1, it, r, s.build_tiles)
                        aggregate(s, it, first and r == 0, last and r == RING - 1)

                five(0, True, False)
                with pe.Fori(1, ROUNDS // RING - 1) as i:
                    five(i, False, False)
                five(ROUNDS // RING - 1, False, True)

                u = Use(s, "xnT1")
                pe.wait_ge(u.free, u.turn)
                hs = [Use(s, f"h{i}") for i in range(HC)]
                for i, u in enumerate(hs):
                    if i < KC:
                        v = Use(s, f"xnT{i}")
                    if not (isinstance(u.before, int) and u.before == 0):
                        pe.wait_ge(u.free, u.before)
                    for k in range(KC):
                        mm3(nc, u.bank[:, 0:ne],
                            (w_root[0][:, k, i * P:(i + 1) * P], w_root[1][:, k, i * P:(i + 1) * P]),
                            (xnT[0][:, k, 0:ne], xnT[1][:, k, 0:ne]), k == 0, False)
                pe.wait_ge(agg_lo, s.g + 1)
                for i, u in enumerate(hs):
                    for k in range(KC):
                        ins = mm3(nc, u.bank[:, 0:ne],
                                  (w_rel[0][:, k, i * P:(i + 1) * P],
                                   w_rel[1][:, k, i * P:(i + 1) * P]),
                                  (agg[0][:, k, 0:ne], agg[1][:, k, 0:ne]), False, k == KC - 1)
                    ins.then_inc(u.ready, 1)

                def gates(j):
                    for q in range(3):
                        u = Use(s, f"{'igo'[q]}{j}")
                        pe.wait_ge(u.free, u.before)
                        c = (q * HC + j) * P
                        for k in range(HC):
                            if j == 0 and q == 0:
                                pe.wait_ge(h_lo, s.g * HC + k + 1)
                            ins = mm3(nc, u.bank[:, 0:ne],
                                      (w_ih[0][:, k, c:c + P], w_ih[1][:, k, c:c + P]),
                                      (hT[0][:, k, 0:ne], hT[1][:, k, 0:ne]), k == 0, k == HC - 1)
                        ins.then_inc(u.ready, 1)

                def pass_turn(name):
                    u = Use(s, name)
                    pe.wait_ge(u.free, u.before)
                    pe.sem_inc(u.ready, 1)
                    pe.sem_inc(u.free, 1)

                gates(0)
                gates(1)
                if s.routes:
                    send_tT(s, TPG)
                else:
                    pass_turn("tT")
                gates(2)
                if s.routes:
                    send_logits(s, TPG)
                else:
                    pass_turn("logits")
                gates(3)
                if s.routes:
                    send_rank(s, TPG)
                else:
                    pass_turn("rank")
                for v in range(s.tiles):
                    u = Use(s, f"fc{v}")
                    pe.wait_ge(u.free, u.before)
                    lo, hi = v * TILE, (v + 1) * TILE
                    for k in range(KC):
                        mm3(nc, u.bank[0:TILE, k * P:(k + 1) * P],
                            (xnT[0][:, k, lo:hi], xnT[1][:, k, lo:hi]),
                            (kv[0][:, k, :], kv[1][:, k, :]), k == 0, False)
                    for k in range(HC):
                        if v == 0:
                            pe.wait_ge(hl_lo, s.g * HC + k + 1)
                        ins = mm3(nc, u.bank[0:TILE, 0:DIM],
                                  (outT[0][:, k, lo:hi], outT[1][:, k, lo:hi]),
                                  (w_fc[0][:, k, :], w_fc[1][:, k, :]), False, k == HC - 1)
                    ins.then_inc(u.ready, 1)

            def before(u):
                if not (isinstance(u.before, int) and u.before == 0):
                    pe.wait_ge(u.free, u.before)

            def send_tT(s, tiles):
                r = s.g + (-1)
                u = Use(s, "tT")
                before(u)
                pe.wait_ge(t_ready, r + 1)
                for v in range(tiles):
                    for k in range(KC):
                        at = (v * KC + k) * TILE
                        ins = t_.transpose(u.bank[:, at:at + TILE],
                                           t_row[:, v, k * P:(k + 1) * P],
                                           ident[0:TILE, 0:TILE])
                ins.then_inc(u.ready, 1)

            def send_logits(s, tiles):
                u, of = Use(s, "logits"), Use(s, "tT")
                before(u)
                pe.wait_ge(of.free, of.turn)
                for v in range(tiles):
                    for k in range(KC):
                        ins = t_.matmul(u.bank[0:TILE, v * EXPERTS:(v + 1) * EXPERTS],
                                        tT[:, v, k, :], w_r[:, k, :], start=(k == 0),
                                        stop=(k == KC - 1))
                ins.then_inc(u.ready, 1)

            def send_rank(s, tiles):
                r = s.g + (-1)
                u = Use(s, "rank")
                before(u)
                pe.wait_ge(sel_ready, r + 1)
                E = EXPERTS
                both = [sel[:, 2, v, :] for v in range(tiles)]
                for v in range(tiles):
                    o = u.bank[0:TILE, v * E:(v + 1) * E]
                    t_.matmul(o, tri[:, :], both[v], start=True, stop=(v == 0))
                    if v:
                        t_.matmul(o, ones[0:TILE, 0:TILE], both[0], start=False, stop=True)
                o = u.bank[0:TILE, TPG * E:(TPG + 1) * E]
                for v in range(tiles):
                    ins = t_.matmul(o, ones[0:TILE, 0:TILE], both[v], start=(v == 0),
                                    stop=(v == tiles - 1))
                ins.then_inc(u.ready, 1)

            each_stage(pe, stage)
            end = Stage(GROUPS, 0, 0, TILES - FULL_GROUPS * TPG, 0, True)
            pe.wait_ge(agg_lo, GROUPS)
            send_tT(end, end.tiles)
            send_logits(end, end.tiles)
            send_rank(end, end.tiles)

        @block.vector
        def _(dve):
            v_ = nc.vector
            me = Steps(dve, dve_step)
            DVE_START = 96
            dve.wait_ge(ld_dst, 16)
            v_.tensor_copy(samp[:, :], dst_raw[:, 0:COLS:STRIDE]).then_inc(samp_ready, 1)

            def stats(c):
                dve.wait_ge(ld_x[c], 16 if c < 4 else 32)
                for i in range(5):
                    ins = v_.bn_stats(bn[:, i, :], xs[:, 5 * c + i, :])
                me.did(ins)
                me.settle()
                for i in range(5):
                    ins = v_.bn_aggr(mv[:, 5 * c + i, :], bn[:, i, :])
                ins.then_inc(mv_ready, 1)
                dve.wait_ge(mv_ready, c + 1)

            for c in range(5):
                stats(c)
            dve.wait_ge(const_ready, 1)
            dve.wait_ge(ld_sampb, 16)
            junk = counts[0:TILE, :, :, :].rearrange("p a b c -> p (a b c)")
            for k in range(SETS):
                ins = v_.tensor_scalar(junk[:, 0:SAMPLES] if k % 2 else
                                       junk[:, SAMPLES + 1:2 * SAMPLES + 1], samp_b[0:TILE, :],
                                       thr[:, k:k + 1], 0.0, ALU.is_lt, ALU.add,
                                       accum_out=cnt[:, k:k + 1])
                me.did(ins)
                me.settle()
            c0, c1 = cnt[:, 0:SETS], cnt[:, SETS:2 * SETS]
            me.did(v_.tensor_scalar(c1, c0, -1.0, float(STRIDE), ALU.add, ALU.mult))
            me.settle()
            me.did(v_.tensor_scalar(c0, c1, 0.0, float(EDGES - RUN), ALU.max, ALU.min))
            me.settle()
            v_.tensor_copy(start[:, :], c0).then_inc(start_ready, 1)
            for c in range(5):
                dve.wait_ge(xnh_ready, c + 1)
                v_.tensor_tensor(xn16[:, 1, 5 * c:5 * c + 5, :], xs_chunk(c),
                                 xn16[:, 0, 5 * c:5 * c + 5, :], ALU.subtract).then_inc(
                                     xnl_ready, 1)
            dve.wait_ge(ld_edges, 160)
            flat = "p k r -> p (k r)"
            es, ed = e_src[:, :, :].rearrange(flat), e_dst[:, :, :].rearrange(flat)
            esf, edf = es.bitcast(F32), ed.bitcast(F32)
            me.did(v_.tensor_scalar(e_blk, es, 7, None, ALU.logical_shift_right))
            me.settle()
            me.did(v_.tensor_scalar(es, es, P - 1, None, ALU.bitwise_and))
            me.settle()
            me.did(v_.tensor_copy(esf, es))
            me.did(v_.tensor_tensor(e_dst[:, :, :].bitcast(F32), e_dst[:, :, :],
                                    thr[:, :].unsqueeze(2).broadcast_to([TILE, SETS, RUN]),
                                    ALU.subtract))
            me.settle()
            me.did(v_.tensor_scalar(e_ok, edf, 0.0, None, ALU.is_ge))
            me.settle()
            me.did(v_.scalar_tensor_tensor(e_ok, edf, float(WIN), e_ok, ALU.is_lt, ALU.mult,
                                           accum_out=n_ok[:, :]))
            me.settle()
            me.did(v_.scalar_tensor_tensor(edf, e_blk, float(WIN), edf, ALU.mult, ALU.add))
            me.settle()
            me.did(v_.scalar_tensor_tensor(edf, edf, 1.0, e_ok, ALU.add, ALU.mult))
            me.settle()
            v_.tensor_scalar(edf, edf, -1.0, None, ALU.add).then_inc(keys_ready, 1)

            for c in range(5):
                v = xs_chunk(c).rearrange("p b (h c) -> p (b h) c", c=HEADC)
                if c:
                    dve.wait_ge(z_ready, c)
                me.did(v_.tensor_reduce(head[:, 2, :], v, AX.X, ALU.add))
                me.settle()
                v_.tensor_scalar(head[:, 0, :], head[:, 2, :], 1.0 / HEADC, None,
                                 ALU.mult).then_inc(head_sum, 1)
                dve.wait_ge(head_sq, c + 1)
                me.did(v_.tensor_reduce(head[:, 2, :], squares.rearrange(
                    "p b (h c) -> p (b h) c", c=HEADC), AX.X, ALU.add))
                me.settle()
                v_.tensor_scalar(head[:, 1, :], head[:, 2, :], 1.0 / (HEADC - 1), None,
                                 ALU.mult).then_inc(head_ss, 1)
                dve.wait_ge(head_std, c + 1)
                me.did(v_.tensor_scalar(head[:, 1, :], head[:, 1, :], 1e-5, None, ALU.add))
                me.settle()
                v_.reciprocal(head[:, 2, :], head[:, 1, :]).then_inc(head_inv, 1)

            b, turn = pro("cols")
            dve.wait_ge(pro_free[b], turn)
            me.did(v_.tensor_tensor(bg[:, :], colsT[:, C_BIH:C_BIH + GATES],
                                    colsT[:, C_BHH:C_BHH + GATES], ALU.add))

            def one_hots(g, tiles):
                T = tiles * HALVES
                with dve.Fori(0, ROUNDS // RING) as i:
                    for r in range(RING):
                        it = i * RING + r
                        n = ROUNDS * g + it
                        dve.wait_ge(cnt_ready, n + 1)
                        at = bass.ds(WPI * HALVES * ROUNDS * g + it * T, T)
                        for to, tab, w in ((oh_a, a_tab, P), (oh_k, k_tab, KEYS)):
                            ins = v_.tensor_tensor(
                                to[:, r, 0:w * T].rearrange("p (a t) -> p a t", t=T),
                                iota_rep[:, 0:w, 0:T],
                                tab[:, at].unsqueeze(1).broadcast_to([P, w, T]),
                                ALU.is_equal)
                        ins.then_inc(oh_ready, 1)

            for k in range(SETS):
                for q in "ak":
                    b, turn = pro(f"{q}{k}")
                    if k >= SETS - 2:
                        dve.wait_ge(pro_free[b], turn)
            one_hots(0, TPG)

            dve.wait_ge(ld_small, 80)
            b0, bs = pro("G0"), pro("S")
            for k in range(KC):
                b, turn = pro(f"G{k}")
                kw, kb = (colsT[:, c + k:c + k + 1] for c in (C_KW, C_KB))
                sl = slice(k * P, (k + 1) * P)
                dve.wait_ge(pro_ready[b], turn)
                dve.wait_ge(pro_ready[bs[0]], bs[1])
                S = gen[bs[0]][:, sl]
                me.did(v_.tensor_tensor(kvt[:, 0, :], S, ident[:, :], ALU.mult))
                me.did(v_.tensor_tensor(kvt[:, 1, :], gen[b][:, 0:P], wv_b[:, sl], ALU.mult))
                me.did(v_.tensor_tensor(kvt[:, 2, :], S, wv_b[:, sl], ALU.mult))
                me.settle()
                me.did(v_.tensor_reduce(sd[:, :], kvt[:, 0, :], AX.X, ALU.add))
                me.settle()
                me.did(v_.scalar_tensor_tensor(kvt[:, 3, :], bv_b[:, sl], sd[:, 0:1],
                                               kvt[:, 1, :], ALU.mult, ALU.add))
                me.did(v_.scalar_tensor_tensor(kvt[:, 0, :], bv_b[:, sl], float(NODES),
                                               kvt[:, 2, :], ALU.mult, ALU.add))
                me.settle()
                me.did(v_.tensor_scalar(kvt[:, 1, :], kvt[:, 0, :], kb, None, ALU.mult))
                me.settle()
                me.did(v_.scalar_tensor_tensor(kvt[:, 2, :], kvt[:, 3, :], kw, kvt[:, 1, :],
                                               ALU.mult, ALU.add))
                me.settle()
                me.did(v_.tensor_tensor(kvt[:, 0, :], kvt[:, 2, :], mask[:, :], ALU.mult))
                me.settle()
                me.did(v_.tensor_tensor(kvt[:, 1, :], kvt[:, 0, :], ident[:, :], ALU.add))
                me.settle()
                me.did(v_.tensor_copy(kv[0][:, k, :], kvt[:, 1, :]))
                me.settle()
                v_.tensor_tensor(kv[1][:, k, :], kvt[:, 1, :], kv[0][:, k, :],
                                 ALU.subtract).then_inc(pro_free[b], 1)
                dve.wait_ge(pro_free[b], turn)
            dve.sem_inc(pro_free[bs[0]], 1)
            for c in range(GATES):
                b, turn = pro(f"w{c}")
                dve.wait_ge(wih_hi, c + 1)
                hi, lo = (w[:, :, c * P:(c + 1) * P] for w in w_ih)
                v_.tensor_tensor(lo, gen[b][:, :].rearrange("p (k n) -> p k n", k=HC), hi,
                                 ALU.subtract).then_inc(pro_free[b], 1)
            dve.sem_inc(kv_ready, 1)
            me.fill(DVE_START)

            def normalise(r, parity, tiles, st):
                def moments(of, turn):
                    for u in range(tiles):
                        ins = v_.bn_stats(bn2[:, u, :], of(u))
                    st.did(ins)
                    st.settle()
                    for u in range(tiles):
                        ins = v_.bn_aggr(mv2[:, u, :], bn2[:, u, :])
                    ins.then_inc(var_ready, 1)
                    dve.wait_ge(var_ready, 2 * r + turn + 1)
                    dve.wait_ge(rs_ready, 2 * r + turn + 1)

                moments(lambda u: x2[:, parity, u, :], 0)
                for u in range(tiles):
                    ins = v_.tensor_scalar(t_row[:, u, :], x2[:, parity, u, :], mv2[:, u, 0:1],
                                           rs2[:, 1, u:u + 1], ALU.subtract, ALU.mult)
                ins.then_inc(t_ready, 1)
                dve.wait_ge(t_ready, r + 1)
                moments(lambda u: t_row[:, u, :], 1)
                if not (isinstance(r, int) and r == 0):
                    dve.wait_ge(scattered, r * (32 * TPG))
                for u in range(tiles):
                    st.did(v_.tensor_scalar(rows[:, u, 0:DIM], t_row[:, u, :], mv2[:, u, 0:1],
                                            rs2[:, 1, u:u + 1], ALU.subtract, ALU.mult))

            def choose(s, r, tiles, st):
                u = Use(s, "logits")
                dve.wait_ge(u.ready, u.turn)
                T = slice(0, tiles)
                v_.tensor_tensor(lg[:, T, :], u.bank[0:TILE, 0:tiles * EXPERTS].rearrange(
                    "p (u e) -> p u e", e=EXPERTS), br_b[:, :].unsqueeze(1).broadcast_to(
                        [TILE, tiles, EXPERTS]), ALU.add).then_inc(u.free, 1)
                dve.wait_ge(u.free, u.turn)
                dve.sem_inc(dve_apart, 1)
                for v in range(tiles):
                    st.did(v_.max(m8[:, v, :], lg[:, v, :]))
                st.settle()
                for v in range(tiles):
                    st.did(v_.max_index(i8[:, v, :], m8[:, v, :], lg[:, v, :]))
                st.settle()
                st.did(v_.tensor_copy(i8f[:, T, :], i8[:, T, 0:2]))
                v_.tensor_tensor(d12[:, T, :], m8[:, T, 0:1], m8[:, T, 1:2],
                                 ALU.subtract).then_inc(d_ready, 1)
                st.settle()
                io = iota8[:, :].unsqueeze(1).broadcast_to([TILE, tiles, EXPERTS])
                for c in range(2):
                    st.did(v_.tensor_tensor(sel[:, c, T, :], io, i8f[:, T, c:c + 1].broadcast_to(
                        [TILE, tiles, EXPERTS]), ALU.is_equal))
                st.settle()
                v_.tensor_tensor(sel[:, 2, T, :], sel[:, 0, T, :], sel[:, 1, T, :],
                                 ALU.add).then_inc(sel_ready, 1)
                st.did(v_.tensor_copy(rows[:, T, DIM:DIM + 1],
                                      ids[:, bass.ds(r * TPG, tiles)].unsqueeze(2)))
                st.did(v_.tensor_copy(rows[:, T, DIM + 1:DIM + 2], i8f[:, T, 0:1]))

            def place(s, r, tiles, st):
                u = Use(s, "rank")
                T, E = slice(0, tiles), EXPERTS
                dve.wait_ge(u.ready, u.turn)
                st.did(v_.tensor_tensor(pos[:, T, :], u.bank[0:TILE, 0:tiles * E].rearrange(
                    "p (u e) -> p u e", e=E), carry[:, :].unsqueeze(1).broadcast_to(
                        [TILE, tiles, E]), ALU.add))
                st.settle()
                v_.tensor_tensor(carry[:, :], carry[:, :],
                                 u.bank[0:TILE, TPG * E:(TPG + 1) * E], ALU.add).then_inc(
                                     u.free, 1)
                dve.wait_ge(u.free, u.turn)
                st.settle()
                for c in range(2):
                    st.did(v_.tensor_tensor(posx[:, c, T, :], pos[:, T, :], sel[:, c, T, :],
                                            ALU.mult))
                st.settle()
                for c in range(2):
                    st.did(v_.tensor_reduce(posf[:, T, c], posx[:, c, T, :], AX.X, ALU.add))
                st.settle()
                v_.tensor_copy(posu[:, T, :], posf[:, T, :]).then_inc(pos_ready, 1)

            def stage(s):
                st = Steps(dve, dve_step, s.g * DVE_STAGE + DVE_START, dve_apart)
                n, r = s.n, s.g + (-1)
                for k in range(KC):
                    u = Use(s, f"xnT{k}")
                    dve.wait_ge(xn_hi, s.g * KC + k + 1)
                    v_.tensor_tensor(xnT[1][:, k, 0:n], u.bank[:, 0:n], xnT[0][:, k, 0:n],
                                     ALU.subtract).then_inc(u.free, 1)
                if s.build_tiles:
                    one_hots(s.g + 1, s.build_tiles)
                dve.wait_ge(agg_hi, s.g + 1)
                for k in range(KC):
                    ins = v_.tensor_tensor(agg[1][:, k, 0:n], ps_agg[k][:, 0:n],
                                           agg[0][:, k, 0:n], ALU.subtract)
                ins.then_inc(agg_lo, 1)
                for i in range(HC):
                    dve.wait_ge(h_hi, s.g * HC + i + 1)
                    v_.tensor_tensor(hT[1][:, i, 0:n], h32[:, i % 2, 0:n], hT[0][:, i, 0:n],
                                     ALU.subtract).then_inc(h_lo, 1)
                if s.routes:
                    normalise(r, 1 - s.parity, TPG, st)

                def cell_out(j):
                    ui, ug, uo = (Use(s, f"{q}{j}") for q in "igo")
                    at = s.g * HC + j + 1
                    dve.wait_ge(ui.free, ui.turn)
                    dve.wait_ge(ug.free, ug.turn)
                    v_.tensor_tensor(cell[:, j % 2, 0, 0:n], gate[:, j % 2, 0, 0:n],
                                     gate[:, j % 2, 1, 0:n], ALU.mult).then_inc(c_ready, 1)
                    dve.wait_ge(tc_ready, at)
                    dve.wait_ge(uo.free, uo.turn)
                    v_.tensor_tensor(out32[:, j % 2, 0:n], gate[:, j % 2, 2, 0:n],
                                     cell[:, j % 2, 1, 0:n], ALU.mult).then_inc(hl_ready, 1)
                    dve.wait_ge(hl_hi, at)
                    v_.tensor_tensor(outT[1][:, j, 0:n], out32[:, j % 2, 0:n],
                                     outT[0][:, j, 0:n], ALU.subtract).then_inc(hl_lo, 1)

                cell_out(0)
                cell_out(1)
                cell_out(2)
                if s.routes:
                    choose(s, r, TPG, st)
                cell_out(3)
                if s.routes:
                    place(s, r, TPG, st)
                dve.wait_ge(ld_rows[s.parity], (s.pair + 1) * 32)
                if not (isinstance(s.pair, int) and s.pair == 0):
                    dve.wait_ge(st_x2[s.parity], s.pair * 16)
                st.did(v_.tensor_tensor(
                    x2[:, s.parity, 0:s.tiles, :], x_row[:, s.parity, 0:s.tiles, :],
                    bfc_b[:, :].unsqueeze(1).broadcast_to([TILE, s.tiles, DIM]), ALU.add))
                st.settle()
                for v in range(s.tiles):
                    u = Use(s, f"fc{v}")
                    dve.wait_ge(u.ready, u.turn)
                    o = x2[:, s.parity, v, :]
                    v_.tensor_tensor(o, o, u.bank[0:TILE, 0:DIM], ALU.add).then_inc(u.free, 1)
                    dve.wait_ge(u.free, u.turn)
                dve.sem_inc(x2_ready, 1)
                st.fill(DVE_STAGE)

            each_stage(dve, stage)
            st = Steps(dve, dve_step, GROUPS * DVE_STAGE + DVE_START)
            end = Stage(GROUPS, 0, 0, TILES - FULL_GROUPS * TPG, 0, True)
            normalise(GROUPS - 1, 0, end.tiles, st)
            choose(end, GROUPS - 1, end.tiles, st)
            place(end, GROUPS - 1, end.tiles, st)


def moe_phase(nc, sem, keep, rows_d, acc_d, W1, W2, b2, out):
    ident, colsT, carry = keep.ident, keep.colsT, keep.carry
    ps_l1, ps_y, ps_x = keep.banks[0:4], keep.banks[4:6], keep.banks[6]
    SUB = SLOTS // P
    LIST = MAXBLK + NODES // SLOTS + 2
    K_BLK, K_BASE, K_END, K_EXP = 0, EXPERTS, 2 * EXPERTS + 1, 3 * EXPERTS + 1
    LAG = 3
    MORE = NODES // SLOTS

    with ExitStack() as ctx:
        m_ = Memory(nc, ctx)
        raw = m_.sbuf("raw_e", [P, 2, 4, RAW], F32)
        w1 = [m_.sbuf(f"w1{q}", [P, 2, KC, FF], F32R) for q in "hl"]
        w2 = [m_.sbuf(f"w2{q}", [P, 2, MC, DIM], F32R) for q in "hl"]
        b2_b = m_.sbuf("b2_b", [P, EXPERTS * DIM], F32)
        x_blk = m_.sbuf("x_blk", [P, SUB, ROW], F32)
        xT32 = m_.sbuf("xT32", [P, KC, SLOTS], F32)
        xT = [m_.sbuf(f"xT{q}", [P, KC, SLOTS], F32R) for q in "hl"]
        g32 = m_.sbuf("g32", [P, 2, SLOTS], F32)
        gT = [m_.sbuf(f"gT{q}", [P, MC, SLOTS], F32R) for q in "hl"]
        y = m_.sbuf("y", [P, SUB, DIM], F32)
        meta = m_.sbuf("meta", [P, SUB, 4], F32)
        first = m_.sbuf("first", [P, SUB], F32)
        part = m_.sbuf("part", [P, 2, SUB], F32)
        wsel = m_.sbuf("wsel", [P, SUB], F32)
        uid = m_.sbuf("uid", [P, SUB], U32)
        e_col = m_.sbuf("e_col", [P, EXPERTS], F32)
        pad = m_.sbuf("pad", [P, SUB, ROW], F32)
        ecap = m_.sbuf("ecap", [1, EXPERTS], F32)
        steps = m_.sbuf("steps", [1, MORE], F32)
        numbers = m_.sbuf("numbers", [1, LIST], F32)
        tabf = m_.sbuf("tabf", [1, K_EXP + LIST], F32)
        tabi = m_.sbuf("tabi", [1, K_EXP + LIST], I32)
        over = m_.sbuf("over", [1, EXPERTS, MORE], F32)
        past = m_.sbuf("past", [1, LIST, EXPERTS], F32)

        moe_const, tab_ready, st_pad, ld_b2, ld_blk = (
            sem(n) for n in ("moe_const", "moe_tab", "st_pad", "ld_b2", "ld_blk"))
        ld_raw_e = [sem(f"ld_raw_e{p}") for p in range(2)]
        w_hi, w_lo = sem("w_hi"), sem("w_lo")
        xt_ready, xt_free, meta_taken, xh_ready, xl_ready = (
            sem(n) for n in ("xt_ready", "xt_free", "meta_taken", "xh_ready", "xl_ready"))
        l1_ready = [sem(f"l1_ready{b}") for b in range(4)]
        l1_free = [sem(f"l1_free{b}") for b in range(4)]
        gh_ready, gl_ready, l2_done, y_free, y_ready, added = (
            sem(n) for n in ("gh_ready", "gl_ready", "l2_done", "y_free", "y_ready", "added"))
        mdve, mpool, mapart, mpapart, st_out = (
            sem(n) for n in ("mdve", "mpool", "mapart", "mpapart", "st_out"))
        block = ctx.enter_context(nc.Block())

        def look(eng, at, lo, hi):
            return eng.value_load(tabi[0:1, at:at + 1], min_val=lo, max_val=hi)

        def experts(eng, start, body, end=None):
            def two(pair):
                for parity in range(2):
                    e = pair * 2 + parity
                    count = eng.value_load(tabi[0:1, bass.ds(e + K_BLK, 1)], min_val=1,
                                           max_val=MORE + 1)
                    base = eng.value_load(tabi[0:1, bass.ds(e + K_BASE, 1)], min_val=0,
                                          max_val=MAXBLK - 1)
                    body(e, pair, parity, base, count)

            eng.wait_ge(tab_ready, 1)
            with eng.Fori(0, EXPERTS // 2 - 1) as pair:
                two(pair)
            two(EXPERTS // 2 - 1)

        @block.sync
        def _(sp):
            def load_raw(e, parity):
                for j in range(4):
                    if j < 2:
                        of = W1[bass.ds(e, 1), j * P:(j + 1) * P, :].rearrange("e p n -> p (e n)")
                        to = raw[:, parity, j, :]
                    else:
                        r = (j - 2) * 4 * P
                        of = W2[bass.ds(e, 1), r:r + 4 * P, :].rearrange(
                            "e (m p) n -> p (e m) n", p=P)
                        to = raw[:, parity, j, :].rearrange("p (m n) -> p m n", m=4)
                    sp.dma_start(to, of).then_inc(ld_raw_e[parity], 16)

            load_raw(0, 0)
            sp.dma_start(b2_b[:, :], b2.rearrange("e n -> (e n)").unsqueeze(0).broadcast_to(
                [P, EXPERTS * DIM])).then_inc(ld_b2, 16)
            sp.wait_ge(tab_ready, 1)
            sp.wait_ge(moe_const, 1)
            for e in range(EXPERTS):
                end = look(sp, K_END + e, e * CAP, e * CAP + NODES)
                sp.dma_start(rows_d[bass.ds(end, SLOTS), :].rearrange("(h p) f -> p h f", p=P),
                             pad[:, :, :]).then_inc(st_pad, 16)
            sp.wait_ge(st_pad, 16 * EXPERTS)

            def load_block(row, n):
                sp.wait_ge(xt_ready, n)
                sp.wait_ge(meta_taken, n)
                sp.dma_start(x_blk[:, :, :], rows_d[bass.ds(row, SLOTS), :].rearrange(
                    "(h p) f -> p h f", p=P)).then_inc(ld_blk, 16)

            def expert(e, pair, parity, base, count):
                if parity == 0:
                    sp.wait_ge(w_lo, pair * 8)
                    load_raw(e + 1, 1)
                else:
                    if not isinstance(e, int):
                        sp.wait_ge(w_lo, pair * 8 + 4)
                        load_raw(e + 1, 0)
                with sp.Fori(0, count) as i:
                    load_block(e * CAP + i * SLOTS, base + i)

            experts(sp, 0, expert)
            total = look(sp, K_BASE + EXPERTS, EXPERTS, MAXBLK)
            load_block(0, total)
            sp.wait_ge(added, total * (16 * SUB))
            sp.dma_start(out, acc_d[0:NODES, :]).then_inc(st_out, 16)
            sp.wait_ge(st_out, 16)

        @block.gpsimd
        def _(pool):
            g_ = nc.gpsimd
            me = Steps(pool, mpool)
            g_.iota(ecap[:, :], pattern=[[CAP, EXPERTS]], base=0, channel_multiplier=0,
                    allow_small_or_imprecise_dtypes=True)
            g_.iota(e_col[:, :], pattern=[[1, EXPERTS]], base=0, channel_multiplier=0,
                    allow_small_or_imprecise_dtypes=True)
            g_.iota(steps[:, :], pattern=[[SLOTS, MORE]], base=SLOTS, channel_multiplier=0,
                    allow_small_or_imprecise_dtypes=True)
            g_.iota(numbers[:, :], pattern=[[1, LIST]], base=0, channel_multiplier=0,
                    allow_small_or_imprecise_dtypes=True)
            me.did(g_.memset(pad[:, :, :], 0.0))
            me.settle()
            g_.iota(pad[:, :, DIM:DIM + 1], pattern=[[P, SUB], [0, 1]], base=NODES,
                    channel_multiplier=1,
                    allow_small_or_imprecise_dtypes=True).then_inc(moe_const, 1)

            def load_hi(e, parity):
                pool.dma_start(w1[0][:, parity, :, :], W1[bass.ds(e, 1), :, :].rearrange(
                    "e (k p) n -> p (e k) n", p=P)).then_inc(w_hi, 16)
                pool.dma_start(w2[0][:, parity, :, :], W2[bass.ds(e, 1), :, :].rearrange(
                    "e (m p) n -> p (e m) n", p=P)).then_inc(w_hi, 16)

            def split(e, pair, parity):
                pool.wait_ge(w_hi, (e + 1) * 32)
                pool.wait_ge(ld_raw_e[parity], (pair + 1) * 64)
                for j in range(4):
                    if j < 2:
                        hi, lo = (w[:, parity, j, :] for w in w1)
                    else:
                        hi, lo = (w[:, parity, 4 * (j - 2):4 * (j - 1), :].rearrange(
                            "p m n -> p (m n)") for w in w2)
                    g_.tensor_tensor(lo, raw[:, parity, j, :], hi, ALU.subtract).then_inc(w_lo, 1)

            load_hi(0, 0)
            split(0, 0, 0)

            def add_block(n):
                for h in range(SUB):
                    at = n * SUB + h
                    pool.wait_ge(y_ready, at + 1)
                    pool.wait_ge(added, at * 16)
                    pool.sem_inc(mpapart, 1)
                    pool.indirect_dma_start(
                        out=acc_d, out_offset=bass.IndirectOffsetOnAxis(ap=uid[:, h:h + 1],
                                                                        axis=0),
                        in_=y[:, h, :], in_offset=None, compute_op=ALU.add).then_inc(added, 16)

            def expert(e, pair, parity, base, count):
                add_block(base)
                if parity == 0:
                    load_hi(e + 1, 1)
                    split(e + 1, pair, 1)
                elif not isinstance(e, int):
                    load_hi(e + 1, 0)
                    split(e + 1, pair + 1, 0)
                with pool.Fori(1, count) as i:
                    add_block(base + i)

            experts(pool, 0, expert)

        @block.scalar
        def _(act):
            a_ = nc.scalar

            def take_x(n):
                e = act.value_load(tabi[0:1, bass.ds(n + K_EXP, 1)], min_val=0,
                                   max_val=EXPERTS - 1)
                act.wait_ge(xt_ready, n + 1)
                act.wait_ge(xl_ready, n)
                for k in range(KC):
                    ins = a_.activation(xT32[:, k, :], ps_x[:, k * SLOTS:(k + 1) * SLOTS],
                                        ACT.Identity,
                                        bias=colsT[:, bass.ds(e * KC + (C_LNB + k), 1)],
                                        scale=colsT[:, bass.ds(e * KC + (C_LNG + k), 1)])
                ins.then_inc(xt_free, 1)

            def split_x(n):
                act.wait_ge(xt_free, n + 1)
                act.wait_ge(l1_ready[3], n * 2)
                a_.activation(xT[0][:, :, :], xT32[:, :, :], ACT.Copy).then_inc(xh_ready, 1)

            act.wait_ge(tab_ready, 1)
            take_x(0)
            split_x(0)

            def expert(e, pair, parity, base, count):
                with act.Fori(0, count) as i:
                    n = base + i
                    for m in range(MC):
                        b = m % 4
                        act.wait_ge(l1_ready[b], n * 2 + (m // 4 + 1))
                        act.wait_ge(gl_ready, n * MC + (m + 1))
                        a_.activation(g32[:, m % 2, :], ps_l1[b][:, 0:SLOTS], ACT.Gelu,
                                      bias=colsT[:, bass.ds(e * MC + (C_B1 + m), 1)]).then_inc(
                                          l1_free[b], 1)
                        act.wait_ge(l1_free[b], n * 2 + (m // 4 + 1))
                        act.wait_ge(l2_done, n * MC + (m + 1))
                        a_.activation(gT[0][:, m, :], g32[:, m % 2, :], ACT.Copy).then_inc(
                            gh_ready, 1)
                        if m == 5:
                            take_x(n + 1)
                    split_x(n + 1)

            experts(act, 0, expert)

        @block.tensor
        def _(pe):
            t_ = nc.tensor
            pe.sem_inc(gl_ready, 2)
            pe.sem_inc(l2_done, MC)

            def transpose_x(n):
                pe.wait_ge(ld_blk, n * 16 + 16)
                pe.wait_ge(xt_free, n)
                for h in range(SUB):
                    for k in range(KC):
                        at = k * SLOTS + h * P
                        ins = t_.transpose(ps_x[:, at:at + P], x_blk[:, h, k * P:(k + 1) * P],
                                           ident[:, :])
                ins.then_inc(xt_ready, 1)

            transpose_x(0)

            def expert(e, pair, parity, base, count):
                pe.wait_ge(w_lo, (e + 1) * 4)
                pe.sem_inc(mapart, 1)
                with pe.Fori(0, count) as i:
                    n = base + i
                    pe.wait_ge(xh_ready, n + 1)
                    pe.wait_ge(xl_ready, n + 1)

                    def layer1(m):
                        b = m % 4
                        pe.wait_ge(l1_free[b], n * 2 + m // 4)
                        c = slice(m * P, (m + 1) * P)
                        for k in range(KC):
                            ins = mm3(nc, ps_l1[b][:, 0:SLOTS],
                                      tuple(w[:, parity, k, c] for w in w1),
                                      tuple(x[:, k, :] for x in xT), k == 0, k == KC - 1)
                        ins.then_inc(l1_ready[b], 1)

                    def layer2(m):
                        if m == 0:
                            pe.wait_ge(y_free, n)
                        pe.wait_ge(gl_ready, n * MC + (m + 3))
                        for h in range(SUB):
                            ins = mm3(nc, ps_y[h][:, 0:DIM],
                                      tuple(g[:, m, h * P:(h + 1) * P] for g in gT),
                                      tuple(w[:, parity, m, :] for w in w2), m == 0,
                                      m == MC - 1)
                        ins.then_inc(l2_done, 1)

                    for m in range(MC):
                        layer1(m)
                        if m >= LAG:
                            layer2(m - LAG)
                        if m == 5:
                            transpose_x(n + 1)
                    for m in range(MC - LAG, MC):
                        layer2(m)

            experts(pe, 0, expert)

        @block.vector
        def _(dve):
            v_ = nc.vector
            me = Steps(dve, mdve)
            dve.wait_ge(moe_const, 1)
            E = EXPERTS
            blk, base_, end_ = (tabf[:, a:a + n] for a, n in (
                (K_BLK, E), (K_BASE, E + 1), (K_END, E)))
            exp = tabf[:, K_EXP:K_EXP + LIST]
            me.did(v_.tensor_copy(end_, carry[0:1, :]))
            me.did(v_.memset(base_[:, 0:1], 0.0))
            me.did(v_.tensor_tensor(ecap[:, :], carry[0:1, :], ecap[:, :], ALU.subtract))
            me.settle()
            me.did(v_.tensor_tensor(over[:, :, :], ecap[:, :].unsqueeze(2).broadcast_to(
                [1, E, MORE]), steps[:, :].unsqueeze(1).broadcast_to([1, E, MORE]), ALU.is_gt))
            me.settle()
            me.did(v_.tensor_reduce(blk, over[:, :, :], AX.X, ALU.add))
            me.settle()
            me.did(v_.tensor_scalar(blk, blk, 1.0, None, ALU.add))
            me.settle()
            for e in range(E):
                me.did(v_.tensor_tensor(base_[:, e + 1:e + 2], base_[:, e:e + 1],
                                        blk[:, e:e + 1], ALU.add))
                me.settle()
            me.did(v_.tensor_tensor(past[:, :, :], numbers[:, :].unsqueeze(2).broadcast_to(
                [1, LIST, E]), base_[:, 0:E].unsqueeze(1).broadcast_to([1, LIST, E]), ALU.is_ge))
            me.settle()
            me.did(v_.tensor_reduce(exp, past[:, :, :], AX.X, ALU.add))
            me.settle()
            me.did(v_.tensor_scalar(exp, exp, -1.0, None, ALU.add))
            me.settle()
            v_.tensor_copy(tabi[:, :], tabf[:, :]).then_inc(tab_ready, 1)

            OUT_STEPS = 8
            START = 40
            me.fill(START)
            dve.wait_ge(ld_b2, 16)

            def split_x(n):
                dve.wait_ge(xh_ready, n + 1)
                v_.tensor_tensor(xT[1][:, :, :], xT32[:, :, :], xT[0][:, :, :],
                                 ALU.subtract).then_inc(xl_ready, 1)

            def take_meta(n):
                dve.wait_ge(ld_blk, n * 16 + 16)
                v_.tensor_copy(meta[:, :, :], x_blk[:, :, DIM:ROW]).then_inc(meta_taken, 1)

            take_meta(0)
            split_x(0)

            def expert(e, pair, parity, base, count):
                with dve.Fori(0, count) as i:
                    n = base + i
                    st = Steps(dve, mdve, n * OUT_STEPS + START)
                    for m in range(MC):
                        dve.wait_ge(gh_ready, n * MC + (m + 1))
                        v_.tensor_tensor(gT[1][:, m, :], g32[:, m % 2, :], gT[0][:, m, :],
                                         ALU.subtract).then_inc(gl_ready, 1)
                    dve.wait_ge(meta_taken, n + 1)
                    st.did(v_.tensor_tensor(first[:, :], meta[:, :, 1],
                                            e_col[:, bass.ds(e, 1)].broadcast_to([P, SUB]),
                                            ALU.is_equal))
                    st.settle()
                    st.did(v_.tensor_tensor(part[:, 0, :], meta[:, :, 2], first[:, :], ALU.mult))
                    st.did(v_.scalar_tensor_tensor(part[:, 1, :], first[:, :], -1.0,
                                                   meta[:, :, 3], ALU.add, ALU.mult))
                    st.settle()
                    st.did(v_.tensor_tensor(wsel[:, :], part[:, 0, :], part[:, 1, :],
                                            ALU.subtract))
                    split_x(n + 1)
                    dve.wait_ge(added, n * (16 * SUB))
                    st.did(v_.tensor_copy(uid[:, :], meta[:, :, 0]))
                    dve.wait_ge(l2_done, n * MC + 2 * MC)
                    for h in range(SUB):
                        ins = v_.tensor_tensor(y[:, h, :], ps_y[h][:, 0:DIM],
                                               b2_b[:, bass.ds(e * DIM, DIM)], ALU.add)
                        if h == 0:
                            st.did(ins)
                        else:
                            ins.then_inc(y_free, 1)
                    st.settle()
                    dve.wait_ge(y_free, n + 1)
                    for h in range(SUB):
                        v_.tensor_scalar(y[:, h, :], y[:, h, :], wsel[:, h:h + 1], None,
                                         ALU.mult).then_inc(y_ready, 1)
                    take_meta(n + 1)
                    st.fill(OUT_STEPS)

            experts(dve, 0, expert)


_INS = ["x", "src", "dst", "L0_gnn_W_rel", "L0_gnn_b_rel", "L0_gnn_W_root", "L0_gnn_W_ih",
        "L0_gnn_W_hh", "L0_gnn_b_ih", "L0_gnn_b_hh", "L0_gnn_W_fc", "L0_gnn_b_fc",
        "L0_mix_kln_weight", "L0_mix_kln_bias", "L0_mix_vln_weight", "L0_mix_vln_bias",
        "L0_ffn_Wr", "L0_ffn_br", "L0_ffn_ln_g", "L0_ffn_ln_b", "L0_ffn_W1", "L0_ffn_b1",
        "L0_ffn_W2", "L0_ffn_b2"]


def kernel(**inputs):
    import concourse.bacc as _bacc
    from concourse.bass_utils import run_bass_kernel_spmd as _run

    nc = _bacc.Bacc("TRN2", target_bir_lowering=False, num_devices=1)
    arrays, args = {}, []
    for name in _INS:
        a = np.ascontiguousarray(inputs[name])
        arrays[f"in_{name}"] = a
        args.append(nc.dram_tensor(f"in_{name}", a.shape, mybir.dt.from_np(a.dtype),
                                   kind="ExternalInput").ap())
    args.append(nc.dram_tensor("out_0", (NODES, DIM), F32, kind="ExternalOutput").ap())
    program(nc, *args)
    r = _run(nc, [arrays], core_ids=[0])
    return r.results[0]["out_0"]
```

```python
import numpy as np
import concourse.bass as bass
from concourse import mybir
from contextlib import ExitStack

F32 = mybir.dt.float32
F32R = mybir.dt.float32r
F16 = mybir.dt.float16
I32 = mybir.dt.int32
U32 = mybir.dt.uint32
ALU = mybir.AluOpType
ACT = mybir.ActivationFunctionType
AX = mybir.AxisListType

NODES, DIM, HID = 3125, 256, 512
EDGES = 103125
EXPERTS, FF = 8, 1024
HEADS, HEADC = 8, 32
P = 128
LN_EPS = 1e-5

TILE = 125
TILES = NODES // TILE
TPG = 2
GROUP = TPG * TILE
FULL_GROUPS = TILES // TPG
GROUPS = FULL_GROUPS + 1
SRC_BLOCKS = -(-NODES // P)
LAST_BLOCK = NODES - (SRC_BLOCKS - 1) * P

WIN = 5
WINDOWS = NODES // WIN
RUN = 256
HALVES = RUN // P
WPI = TPG
ROUNDS = GROUP // (WIN * WPI)
RING = 5
EARLY = 2
LATE = [[10, 11, 12], [13, 14, 15, 16], [17, 18, 19, 20], [21, 22, 23, 24]]
SETS = WINDOWS // TILE
STRIDE = 33
SAMPLES = EDGES // STRIDE
COLS = EDGES // TILE
KEYS = WIN * SRC_BLOCKS
SPAN = 5 * TILE
SPANS = NODES // SPAN

SLOTS = 256
CAP = NODES + SLOTS + 3
ROW = DIM + 4
MAXBLK = 2 * NODES // SLOTS + EXPERTS
KC, HC, MC = DIM // P, HID // P, FF // P
GATES = 3 * HC
RAW = 1024

C_B1, C_LNG, C_LNB = 0, EXPERTS * MC, EXPERTS * MC + EXPERTS * KC
C_BREL = C_LNB + EXPERTS * KC
C_BIH = C_BREL + HC
C_BHH = C_BIH + GATES
C_KW = C_BHH + GATES
C_KB = C_KW + KC

USES = (["xnT0", "xnT1"] + [f"h{m}" for m in range(HC)]
        + [f"{q}{j}" for j in range(2) for q in "igo"] + ["tT"]
        + [f"{q}2" for q in "igo"] + ["logits"] + [f"{q}3" for q in "igo"]
        + ["rank", "fc0", "fc1"])
BANKS = 4


class Steps:

    def __init__(self, eng, sem, base=0, apart=None):
        self.eng, self.sem, self.base, self.n, self.apart = eng, sem, base, 0, apart

    def did(self, ins):
        ins.then_inc(self.sem, 1)
        self.n += 1

    def settle(self):
        self.eng.wait_ge(self.sem, self.base + self.n)
        if self.apart is not None:
            self.eng.sem_inc(self.apart, 1)

    def fill(self, total):
        assert self.n <= total, self.n
        if self.n < total:
            self.eng.sem_inc(self.sem, total - self.n)


class Stage:

    def __init__(self, g, pair, parity, tiles, build_tiles, routes):
        self.g, self.pair, self.parity, self.tiles = g, pair, parity, tiles
        self.build_tiles, self.routes = build_tiles, routes
        self.n = tiles * TILE
        self.even = self.n + self.n % 2


def bank_of(use):
    return USES.index(use) % BANKS


def bank_turn(g, use):
    b, at = bank_of(use), USES.index(use)
    per_stage = len(USES[b::BANKS])
    return g * per_stage + at // BANKS + 1


def each_stage(eng, body):
    body(Stage(0, 0, 0, TPG, TPG, False))
    with eng.Fori(0, (FULL_GROUPS - 2) // 2) as i:
        body(Stage(2 * i + 1, i, 1, TPG, TPG, True))
        body(Stage(2 * i + 2, i + 1, 0, TPG, TPG, True))
    g = FULL_GROUPS - 1
    body(Stage(g, g // 2, g % 2, TPG, TILES - FULL_GROUPS * TPG, True))
    body(Stage(g + 1, (g + 1) // 2, (g + 1) % 2, TILES - FULL_GROUPS * TPG, 0, True))


DVE_STAGE = 64
POOL_STAGE = 16


def program(nc, x, src, dst, W_rel, b_rel, W_root, W_ih, W_hh, b_ih, b_hh, W_fc, b_fc,
            kln_w, kln_b, vln_w, vln_b, Wr, br, ln_g, ln_b, W1, b1, W2, b2, out):
    samp_d = nc.dram_tensor("samp_d", [SAMPLES], F32).ap()
    ends_d = [nc.dram_tensor(f"{q}_d", [-(-EDGES // RUN) * RUN], I32).ap() for q in ("dst", "src")]
    xn_d = nc.dram_tensor("xn_d", [NODES, DIM], F32).ap()
    rows_d = nc.dram_tensor("rows_d", [EXPERTS * CAP, ROW], F32).ap()
    sums_d = nc.dram_tensor("sums_d", [NODES, DIM], F32).ap()
    acc_d = nc.dram_tensor("acc_d", [NODES + SLOTS, DIM], F32).ap()

    with ExitStack() as ctx:
        def sem(name):
            return ctx.enter_context(nc.semaphore(name))

        keep = Memory(nc, ctx)
        keep.ident = keep.sbuf("ident", [P, P], F32)
        keep.colsT = keep.sbuf("colsT", [P, P], F32)
        keep.carry = keep.sbuf("carry", [TILE, EXPERTS], F32)
        keep.raw = keep.sbuf("raw", [P, 2, RAW], F32)
        keep.banks = [ctx.enter_context(nc.psum_tensor(f"bank{i}", [P, 512], F32))
                      for i in range(8)]
        gnn_phase(nc, sem, keep, samp_d, ends_d, xn_d, sums_d, rows_d, acc_d, x, src, dst, W_rel, b_rel, W_root,
                  W_ih, b_ih, b_hh, W_fc, b_fc, kln_w, kln_b, vln_w, vln_b, Wr, br, ln_g, ln_b,
                  b1)
        moe_phase(nc, sem, keep, rows_d, acc_d, W1, W2, b2, out)


class Memory:

    def __init__(self, nc, stack):
        self.nc, self.stack = nc, stack

    def sbuf(self, name, shape, dt):
        return self.stack.enter_context(self.nc.sbuf_tensor(name, shape, dt))


def mm3(nc, out, lhs, rhs, start, stop):
    (lh, ll), (rh, rl) = lhs, rhs
    nc.tensor.matmul(out, lh, rh, start=start, stop=False)
    nc.tensor.matmul(out, lh, rl, start=False, stop=False)
    return nc.tensor.matmul(out, ll, rh, start=False, stop=stop)


def gnn_phase(nc, sem, keep, samp_d, ends_d, xn_d, sums_d, rows_d, acc_d, x, src, dst, W_rel, b_rel, W_root,
              W_ih, b_ih, b_hh, W_fc, b_fc, kln_w, kln_b, vln_w, vln_b, Wr, br, ln_g, ln_b, b1):
    ident, colsT, carry, raw = keep.ident, keep.colsT, keep.carry, keep.raw
    gen, ps_cnt, ps_agg = keep.banks[0:4], keep.banks[4:6], keep.banks[6:8]

    with ExitStack() as ctx:
        m = Memory(nc, ctx)
        ones = m.sbuf("ones", [P, P], F32)
        tri = m.sbuf("tri", [TILE, TILE], F32)
        iota8 = m.sbuf("iota8", [TILE, EXPERTS], F32)
        iota_rep = m.sbuf("iota_rep", [P, P, WPI * HALVES], F16)
        ids = m.sbuf("ids", [TILE, TILES], F32)
        half_pow = m.sbuf("half_pow", [P, 1, 5], F32)
        xn16 = m.sbuf("xn16", [P, 2, SRC_BLOCKS, DIM], F16)
        w_rel = [m.sbuf(f"w_rel{q}", [P, KC, HID], F32R) for q in "hl"]
        w_root = [m.sbuf(f"w_root{q}", [P, KC, HID], F32R) for q in "hl"]
        w_fc = [m.sbuf(f"w_fc{q}", [P, HC, DIM], F32R) for q in "hl"]
        w_ih = [m.sbuf(f"w_ih{q}", [P, HC, GATES * P], F32R) for q in "hl"]
        kv = [m.sbuf(f"kv{q}", [P, KC, P], F32R) for q in "hl"]
        w_r = m.sbuf("w_r", [P, KC, EXPERTS], F32)
        br_b = m.sbuf("br_b", [TILE, EXPERTS], F32)
        bfc_b = m.sbuf("bfc_b", [TILE, DIM], F32)
        bg = m.sbuf("bg", [P, GATES], F32)
        counts = m.sbuf("counts", [P, 2, SRC_BLOCKS, GROUP], F16)
        a_tab = m.sbuf("a_tab", [P, WINDOWS * HALVES], F16)
        k_tab = m.sbuf("k_tab", [P, WINDOWS * HALVES], F16)
        oh_a = m.sbuf("oh_a", [P, RING, P * WPI * HALVES], F16)
        oh_k = m.sbuf("oh_k", [P, RING, KEYS * WPI * HALVES], F16)

        covered = m.sbuf("covered", [TILE, 1], F32)
        runs_f = m.sbuf("runs_f", [1, 1], F32)
        runs = m.sbuf("runs", [1, 1], I32)
        extra = raw[0:TILE, 0, 0:TPG * DIM].rearrange("p (u f) -> p u f", u=TPG)

        with ExitStack() as early:
            e = Memory(nc, early)
            samp_b = e.sbuf("samp_b", [P, SAMPLES], F32)
            xs = e.sbuf("xs", [P, SRC_BLOCKS, DIM], F32)
            dst_raw = e.sbuf("dst_raw", [TILE, COLS], I32)
            samp = e.sbuf("samp", [TILE, SAMPLES // TILE], F32)
            e_dst = e.sbuf("e_dst", [TILE, SETS, RUN], I32)
            e_src_all = e.sbuf("e_src", [P, SETS, RUN], I32)
            e_src = e_src_all[0:TILE, :, :]
            e_blk = samp_b[0:TILE, 0:SETS * RUN].bitcast(I32)
            e_ok = samp_b[0:TILE, SETS * RUN:2 * SETS * RUN]
            thr = e.sbuf("thr", [TILE, SETS], F32)
            cnt = e.sbuf("cnt", [TILE, 2 * SETS], F32)
            start = e.sbuf("start", [TILE, SETS], U32)
            n_ok = e.sbuf("n_ok", [TILE, 1], F32)
            bn = e.sbuf("bn", [P, 5, 6], F32)
            mv = e.sbuf("mv", [P, SRC_BLOCKS, 2], F32)
            rstd = e.sbuf("rstd", [P, 2, SRC_BLOCKS], F32)
            head = e.sbuf("head", [P, 3, SRC_BLOCKS * HEADS], F32)
            prow = e.sbuf("prow", [P, P], F32)
            mask = e.sbuf("mask", [P, P], F32)
            wv_b = e.sbuf("wv_b", [P, DIM], F32)
            bv_b = e.sbuf("bv_b", [P, DIM], F32)
            kvt = e_src_all[:, 0:5, :].rearrange("p a (b c) -> p (a b) c", c=P).bitcast(F32)
            sd = e.sbuf("sd", [P, KC], F32)
            squares = [samp_b[:, a * 5 * DIM:(a + 1) * 5 * DIM].rearrange(
                "p (b f) -> p b f", f=DIM) for a in range(2)]
            zsum = squares[0]
        with ExitStack() as general:
            e = Memory(nc, general)
            e.sbuf("first_rows", [TILE, 2, 2, TPG, DIM], F32)
            all_src = e.sbuf("all_src", [TILE, COLS], I32)
            all_dst = e.sbuf("all_dst", [TILE, COLS], I32)
            dst_f = e.sbuf("dst_f", [TILE, COLS], F32)
            span = e.sbuf("span", [TILE, SPAN], F32)
            oh_dst = e.sbuf("oh_dst", [TILE, SPAN], F32)
            src_at = e.sbuf("src_at", [TILE, 1], U32)
            src_rows = e.sbuf("src_rows", [TILE, DIM], F32)
            sums = e.sbuf("sums", [TILE, SPAN // TILE, DIM], F32)
            ps_sums = gen + ps_agg[0:1]
        x_row = m.sbuf("x_row", [TILE, 2, TPG, DIM], F32)
        xn_row = m.sbuf("xn_row", [TILE, 2, TPG, DIM], F32)
        agg = [m.sbuf(f"agg{q}", [P, KC, GROUP], F32R) for q in "hl"]
        xnT = [m.sbuf(f"xnT{q}", [P, KC, GROUP], F32R) for q in "hl"]
        h32 = m.sbuf("h32", [P, 2, GROUP], F32)
        hT = [m.sbuf(f"hT{q}", [P, HC, GROUP], F32R) for q in "hl"]
        gate = m.sbuf("gate", [P, 2, 3, GROUP], F32)
        cell = m.sbuf("cell", [P, 2, 2, GROUP], F32)
        out32 = h32
        outT = [m.sbuf(f"outT{q}", [P, HC, GROUP], F32R) for q in "hl"]
        x2 = m.sbuf("x2", [TILE, 2, TPG, DIM], F32)
        t_row = m.sbuf("t_row", [TILE, TPG, DIM], F32)
        rows = m.sbuf("rows", [TILE, TPG, ROW], F32)
        tT = m.sbuf("tT", [P, TPG, KC, TILE], F32)
        bn2 = m.sbuf("bn2", [TILE, TPG, 6], F32)
        mv2 = m.sbuf("mv2", [TILE, TPG, 2], F32)
        rs2 = m.sbuf("rs2", [TILE, 2, TPG], F32)
        lg = m.sbuf("lg", [TILE, TPG, EXPERTS], F32)
        m8 = m.sbuf("m8", [TILE, TPG, 8], F32)
        i8 = m.sbuf("i8", [TILE, TPG, 8], U32)
        i8f = m.sbuf("i8f", [TILE, TPG, 2], F32)
        d12 = m.sbuf("d12", [TILE, TPG, 1], F32)
        sel = m.sbuf("sel", [TILE, 3, TPG, EXPERTS], F32)
        pos = m.sbuf("pos", [TILE, TPG, EXPERTS], F32)
        posx = m.sbuf("posx", [TILE, 2, TPG, EXPERTS], F32)
        posf = m.sbuf("posf", [TILE, TPG, 2], F32)
        posu = m.sbuf("posu", [TILE, TPG, 2], U32)

        ld_dst, ld_par, ld_small, ld_sampb, st_samp = (
            sem(n) for n in ("ld_dst", "ld_par", "ld_small", "ld_sampb", "st_samp"))
        ld_x = [sem(f"ld_x{c}") for c in range(5)]
        ld_raw = [sem(f"ld_raw{c}") for c in range(2)]
        ld_whi, ld_edges, st_xn = (
            sem(n) for n in ("ld_whi", "ld_edges", "st_xn"))
        st_ends = sem("st_ends")
        pad_ready, const_ready, samp_ready, start_ready = (
            sem(n) for n in ("pad_ready", "const_ready", "samp_ready", "start_ready"))
        mv_ready, rstd_ready, xn_ready, xnh_ready, xnl_ready = (
            sem(n) for n in ("mv_ready", "rstd_ready", "xn_ready", "xnh_ready", "xnl_ready"))
        head_sum, head_dev, head_sq, head_ss, head_std, head_inv, z_ready = (
            sem(n) for n in ("head_sum", "head_dev", "head_sq", "head_ss", "head_std",
                             "head_inv", "z_ready"))
        keys_ready, tab_ready, wlo_ready, raw_used, wih_hi, cols_ready, kv_ready = (
            sem(n) for n in ("keys_ready", "tab_ready", "wlo_ready", "raw_used", "wih_hi",
                             "cols_ready", "kv_ready"))
        zz_ready, zsum_ready = sem("zz_ready"), sem("zsum_ready")
        pro_ready = [sem(f"pro_ready{b}") for b in range(BANKS)]
        pro_free = [sem(f"pro_free{b}") for b in range(BANKS)]
        oh_ready, cnt_ready, cnt_taken, agg_ready, agg_hi, agg_lo = (
            sem(n) for n in ("oh_ready", "cnt_ready", "cnt_taken", "agg_ready",
                             "agg_hi", "agg_lo"))
        gready = [sem(f"gready{b}") for b in range(BANKS)]
        gfree = [sem(f"gfree{b}") for b in range(BANKS)]
        ld_rows = [sem(f"ld_rows{b}") for b in range(2)]
        st_x2 = [sem(f"st_x2{b}") for b in range(2)]
        xn_hi, h_hi, h_lo, c_ready, tc_ready, hl_ready, hl_hi, hl_lo, x2_ready = (
            sem(n) for n in ("xn_hi", "h_hi", "h_lo", "c_ready", "tc_ready", "hl_ready",
                             "hl_hi", "hl_lo", "x2_ready"))
        var_ready, rs_ready, t_ready, d_ready, w_ready, sel_ready, pos_ready, scattered = (
            sem(n) for n in ("var_ready", "rs_ready", "t_ready", "d_ready", "w_ready",
                             "sel_ready", "pos_ready", "scattered"))
        dve_step, pool_step = sem("dve_step"), sem("pool_step")
        dve_apart, pool_apart, sp_apart = sem("dve_apart"), sem("pool_apart"), sem("sp_apart")
        end_ready, end_free = sem("end_ready"), sem("end_free")
        ok_counted, ok_summed, runs_ready, ld_all, span_ready, dst_step = (
            sem(n) for n in ("ok_counted", "ok_summed", "runs_ready", "ld_all", "span_ready",
                             "dst_step"))
        gathered = [sem(f"gathered{r}") for r in range(RING)]
        src_at_ready, oh_dst_ready, summed, sums_ready, st_sums, ld_extra = (
            sem(n) for n in ("src_at_ready", "oh_dst_ready", "summed",
                             "sums_ready", "st_sums", "ld_extra"))

        def general_runs(eng):
            eng.wait_ge(runs_ready, 1)
            return eng.value_load(runs[0:1, 0:1], min_val=0, max_val=1)

        PRO = (["cols"] + [f"{q}{k}" for k in range(SETS) for q in "ak"]
               + [f"w{c}" for c in range(GATES)])
        ps_zz = [ps_agg[0][:, k * P:(k + 1) * P] for k in range(KC)]
        ps_zsum = ps_agg[1][:, 0:DIM]

        def pro(use):
            at = PRO.index(use)
            return at % BANKS, at // BANKS + 1

        ENDS = ["tT", "logits", "rank"]

        class Use:

            def __init__(self, s, name):
                if isinstance(s.g, int) and s.g == GROUPS:
                    n = ENDS.index(name)
                    self.bank, self.ready, self.free = ps_agg[n % 2], end_ready, end_free
                    self.turn, self.before = n + 1, n
                else:
                    b = bank_of(name)
                    self.bank, self.ready, self.free = gen[b], gready[b], gfree[b]
                    self.turn = bank_turn(s.g, name)
                    self.before = bank_turn(s.g, name) - 1 if isinstance(s.g, int) else \
                        bank_turn(s.g, name) + (-1)

        block = ctx.enter_context(nc.Block())
        dst_v = dst.rearrange("(p c) -> p c", p=TILE)

        def xs_chunk(c):
            return xs[:, 5 * c:5 * c + 5, :]

        @block.sync
        def _(sp):
            sp.dma_start(dst_raw[:, :], dst_v).then_inc(ld_dst, 16)
            for to, of in zip(ends_d, (dst, src)):
                sp.dma_start(to[0:EDGES].rearrange("(p c) -> p c", p=TILE),
                             of.rearrange("(p c) -> p c", p=TILE)).then_inc(st_ends, 16)
            for c in range(5):
                if c < 4:
                    sp.dma_start(xs_chunk(c), x[640 * c:640 * c + 640, :].rearrange(
                        "(b p) f -> p b f", p=P)).then_inc(ld_x[c], 16)
                else:
                    sp.wait_ge(pad_ready, 1)
                    sp.dma_start(xs[:, 20:24, :], x[2560:3072, :].rearrange(
                        "(b p) f -> p b f", p=P)).then_inc(ld_x[c], 16)
                    sp.dma_start(xs[0:LAST_BLOCK, 24, :], x[3072:NODES, :]).then_inc(ld_x[c], 16)
                if c == 0:
                    sp.wait_ge(samp_ready, 1)
                    sp.dma_start(samp_d.rearrange("(p c) -> p c", p=TILE), samp[:, :]).then_inc(
                        st_samp, 16)
                    sp.wait_ge(st_samp, 16)
                    sp.dma_start(samp_b[0:TILE, :], samp_d.unsqueeze(0).broadcast_to(
                        [TILE, SAMPLES])).then_inc(ld_sampb, 16)
            for at, n, a in ((C_B1, 64, b1.rearrange("e (m c) -> (e m) c", c=P)),
                             (C_LNG, 16, ln_g.rearrange("e (k c) -> (e k) c", c=P)),
                             (C_LNB, 16, ln_b.rearrange("e (k c) -> (e k) c", c=P)),
                             (C_BREL, HC, b_rel.rearrange("(m c) -> m c", c=P)),
                             (C_BIH, HC, b_ih[0:HID].rearrange("(m c) -> m c", c=P)),
                             (C_BIH + HC, 2 * HC, b_ih[2 * HID:4 * HID].rearrange(
                                 "(m c) -> m c", c=P)),
                             (C_BHH, HC, b_hh[0:HID].rearrange("(m c) -> m c", c=P)),
                             (C_BHH + HC, 2 * HC, b_hh[2 * HID:4 * HID].rearrange(
                                 "(m c) -> m c", c=P)),
                             (C_KW, KC, kln_w.rearrange("(k h) o c -> k (h o c)", k=KC)),
                             (C_KB, KC, kln_b.rearrange("(k h) o c -> k (h o c)", k=KC))):
                sp.dma_start(prow[at:at + n, :], a).then_inc(ld_par, 16)
            sp.dma_start(wv_b[:, :], vln_w.rearrange("h o c -> o (h c)").broadcast_to(
                [P, DIM])).then_inc(ld_small, 16)
            sp.dma_start(bv_b[:, :], vln_b.rearrange("h o c -> o (h c)").broadcast_to(
                [P, DIM])).then_inc(ld_small, 16)
            sp.dma_start(bfc_b[:, :], b_fc.unsqueeze(0).broadcast_to([TILE, DIM])).then_inc(
                ld_small, 16)
            sp.dma_start(w_r[:, :, :], Wr.rearrange("(k p) e -> p k e", p=P)).then_inc(
                ld_small, 16)
            for c in range(5):
                sp.wait_ge(xn_ready, c + 1)
                if c < 4:
                    sp.dma_start(xn_d[640 * c:640 * c + 640, :].rearrange(
                        "(b p) f -> p b f", p=P), xs_chunk(c)).then_inc(st_xn, 16)
                else:
                    sp.dma_start(xn_d[2560:3072, :].rearrange("(b p) f -> p b f", p=P),
                                 xs[:, 20:24, :]).then_inc(st_xn, 16)
                    sp.dma_start(xn_d[3072:NODES, :], xs[0:LAST_BLOCK, 24, :]).then_inc(
                        st_xn, 16)
            items = [W_rel.rearrange("(k p) n -> p k n", p=P),
                     W_root.rearrange("(k p) n -> p k n", p=P),
                     W_fc.rearrange("(k p) n -> p k n", p=P)]
            for c in range(0, GATES, 2):
                row = HID * (0, 2, 3)[c // HC] + P * (c % HC)
                items.append(W_ih[row:row + 2 * P, :].rearrange("(c p) n -> p c n", p=P))
            for j, item in enumerate(items):
                if 2 <= j < 5:
                    sp.wait_ge(wlo_ready, j - 1)
                elif j >= 5:
                    sp.wait_ge(raw_used, j - 4)
                k = item.shape[1]
                sp.dma_start(raw[:, j % 2, :].rearrange("p (k n) -> p k n", k=k), item).then_inc(
                    ld_raw[j % 2], 16)

            runs_sp = general_runs(sp)

            def load_extra(g, tiles):
                with sp.If(runs_sp > 0):
                    if not (isinstance(g, int) and g == 0):
                        sp.wait_ge(agg_ready, g)
                    sp.dma_start(extra[:, 0:tiles, :], sums_d[bass.ds(g * GROUP, tiles * TILE), :]
                                 .rearrange("(u p) f -> p u f", p=TILE)).then_inc(ld_extra, 16)

            def load_rows(g, parity, tiles):
                n = tiles * TILE
                sp.dma_start(xn_row[:, parity, 0:tiles, :], xn_d[bass.ds(g * GROUP, n), :]
                             .rearrange("(u p) f -> p u f", p=TILE)).then_inc(ld_rows[parity], 16)
                sp.dma_start(x_row[:, parity, 0:tiles, :], x[bass.ds(g * GROUP, n), :]
                             .rearrange("(u p) f -> p u f", p=TILE)).then_inc(ld_rows[parity], 16)

            sp.wait_ge(st_xn, 96)
            sp.wait_ge(zz_ready, 1)
            load_rows(0, 0, TPG)
            sp.wait_ge(kv_ready, 1)
            with sp.If(runs_sp > 0):
                for to, of in ((all_src, src), (all_dst, dst)):
                    sp.dma_start(to[:, :], of.rearrange("(p c) -> p c", p=TILE)).then_inc(
                        ld_all, 16)
                sp.sem_inc(st_sums, 16)
                with sp.Fori(0, SPANS) as i:
                    sp.wait_ge(sums_ready, (i + 2) * (SPAN // TILE))
                    sp.dma_start(sums_d[bass.ds(i * SPAN, SPAN), :].rearrange(
                        "(u p) f -> p u f", p=TILE), sums[:, :, :]).then_inc(st_sums, 16)
                sp.wait_ge(st_sums, 16 * SPANS + 16)
            load_extra(0, TPG)

            def stage(s):
                if s.build_tiles:
                    if not (isinstance(s.g, int) and s.g == 0):
                        sp.wait_ge(x2_ready, s.g)
                        sp.sem_inc(sp_apart, 1)
                    load_extra(s.g + 1, s.build_tiles)
                    load_rows(s.g + 1, 1 - s.parity, s.build_tiles)
                sp.wait_ge(x2_ready, s.g + 1)
                sp.dma_start(acc_d[bass.ds(s.g * GROUP, s.n), :].rearrange(
                    "(u p) f -> p u f", p=TILE), x2[:, s.parity, 0:s.tiles, :]).then_inc(
                        st_x2[s.parity], 16)

            for b in range(2):
                sp.sem_inc(st_x2[b], 16)
            each_stage(sp, stage)
            sp.wait_ge(st_x2[0], 16 * ((GROUPS + 1) // 2) + 16)
            sp.wait_ge(st_x2[1], 16 * (GROUPS // 2) + 16)

        @block.gpsimd
        def _(pool):
            g_ = nc.gpsimd
            me = Steps(pool, pool_step)
            g_.memset(xs[:, SRC_BLOCKS - 1, :], 0.0).then_inc(pad_ready, 1)
            g_.memset(half_pow[:, 0, :], -0.5)
            g_.iota(thr[:, :], pattern=[[WIN * TILE, SETS]], base=0, channel_multiplier=WIN,
                    allow_small_or_imprecise_dtypes=True)
            me.did(g_.memset(ident[:, :], 0.0))
            me.settle()
            g_.affine_select(out=ident[:, :], in_=ident[:, :], compare_op=ALU.not_equal, fill=1.0,
                             base=0, pattern=[[-1, P]], channel_multiplier=1)
            g_.memset(ones[:, :], 1.0)
            g_.iota(iota8[:, :], pattern=[[1, EXPERTS]], base=0, channel_multiplier=0,
                    allow_small_or_imprecise_dtypes=True)
            g_.iota(carry[:, :], pattern=[[CAP, EXPERTS]], base=0, channel_multiplier=0,
                    allow_small_or_imprecise_dtypes=True)
            g_.iota(ids[:, :], pattern=[[TILE, TILES]], base=0, channel_multiplier=1,
                    allow_small_or_imprecise_dtypes=True)
            g_.iota(iota_rep[:, :, :], pattern=[[1, P], [0, WPI * HALVES]], base=0,
                    channel_multiplier=0, allow_small_or_imprecise_dtypes=True)
            me.did(g_.memset(mask[:, :], 0.0))
            me.settle()
            for q in range(P // HEADC):
                me.did(g_.memset(mask[HEADC * q:HEADC * q + HEADC,
                                      HEADC * q:HEADC * q + HEADC], 1.0 / NODES))
                me.settle()
            me.did(g_.memset(tri[:, :], 1.0))
            me.settle()
            g_.affine_select(out=tri[:, :], in_=tri[:, :], compare_op=ALU.is_gt, fill=0.0,
                             base=0, pattern=[[1, TILE]], channel_multiplier=-1).then_inc(
                                 const_ready, 1)
            for hi, w in ((w_rel[0], W_rel), (w_root[0], W_root), (w_fc[0], W_fc)):
                pool.dma_start(hi[:, :, :], w.rearrange("(k p) n -> p k n", p=P)).then_inc(
                    ld_whi, 16)
            pool.dma_start(br_b[:, :], br.unsqueeze(0).broadcast_to([TILE, EXPERTS])).then_inc(
                scattered, 16)
            for c in range(5):
                pool.wait_ge(mv_ready, c + 1)
                r = rstd[:, 0, 5 * c:5 * c + 5]
                q = rstd[:, 1, 5 * c:5 * c + 5]
                me.did(g_.tensor_scalar(q, mv[:, 5 * c:5 * c + 5, 1], LN_EPS, None, ALU.add))
                me.settle()
                me.did(g_.tensor_tensor(r, q, half_pow[:, 0, 0:5], ALU.pow))
                me.settle()
                me.did(g_.tensor_tensor(q, mv[:, 5 * c:5 * c + 5, 0], r, ALU.mult))
                me.settle()
                g_.tensor_scalar(q, q, -1.0, None, ALU.mult).then_inc(rstd_ready, 1)
            pool.wait_ge(start_ready, 1)
            pool.wait_ge(st_ends, 32)
            for k in range(SETS):
                for to, of in zip((e_dst, e_src), ends_d):
                    table = of.rearrange("(a b) -> a b", b=RUN)
                    pool.indirect_dma_start(
                        out=to[:, k, :], out_offset=None, in_=table,
                        in_offset=bass.IndirectOffsetOnAxis(ap=start[:, k:k + 1], axis=1)
                    ).then_inc(ld_edges, 16)
            def by_head(c, row):
                return head[:, row, c * 5 * HEADS:(c + 1) * 5 * HEADS].unsqueeze(2).broadcast_to(
                    [P, 5 * HEADS, HEADC])

            pool.wait_ge(head_sum, 1)
            pool.wait_ge(st_xn, 96)
            for c in range(5):
                v = xs_chunk(c).rearrange("p b (h c) -> p (b h) c", c=HEADC)
                g_.tensor_tensor(v, v, by_head(c, 0), ALU.subtract).then_inc(head_dev, 1)
            pool.wait_ge(ld_whi, 48)
            for j, (hi, lo) in enumerate((w_rel, w_root, w_fc)):
                pool.wait_ge(ld_raw[j % 2], 16 * (j // 2 + 1))
                g_.tensor_tensor(lo[:, :, :].rearrange("p k n -> p (k n)"), raw[:, j % 2, :],
                                 hi[:, :, :].rearrange("p k n -> p (k n)"),
                                 ALU.subtract).then_inc(wlo_ready, 1)
            pool.wait_ge(head_inv, 1)
            pool.wait_ge(head_dev, 5)
            for c in range(5):
                v = xs_chunk(c).rearrange("p b (h c) -> p (b h) c", c=HEADC)
                g_.tensor_tensor(v, v, by_head(c, 2), ALU.mult).then_inc(z_ready, 1)
            for c in range(1, 5):
                pool.wait_ge(z_ready, c + 1)
                if c > 1:
                    pool.wait_ge(zsum_ready, c - 1)
                g_.tensor_tensor(zsum, zsum if c > 1 else xs_chunk(0), xs_chunk(c),
                                 ALU.add).then_inc(zsum_ready, 1)
            with pool.If(general_runs(pool) > 0):
                pool.wait_ge(ld_all, 32)
                g_.iota(span[:, :], pattern=[[1, SPAN]], base=0, channel_multiplier=0,
                        allow_small_or_imprecise_dtypes=True).then_inc(span_ready, 1)
                with pool.Fori(0, SPANS * COLS // RING) as t:
                    for r in range(RING):
                        pool.wait_ge(src_at_ready, t * RING + (r + 1))
                        pool.sem_inc(pool_apart, 1)
                        pool.indirect_dma_start(
                            out=src_rows[:, :], out_offset=None, in_=xn_d,
                            in_offset=bass.IndirectOffsetOnAxis(ap=src_at[:, 0:1], axis=0)
                        ).then_inc(gathered[r], 16)

            def route(s, r, parity, tiles):
                st = Steps(pool, pool_step, r * POOL_STAGE + POOL_START, pool_apart)
                for turn in range(2):
                    pool.wait_ge(var_ready, 2 * r + turn + 1)
                    pool.sem_inc(pool_apart, 1)
                    st.did(g_.tensor_scalar(rs2[:, 0, 0:tiles], mv2[:, 0:tiles, 1], LN_EPS, None,
                                            ALU.add))
                    st.settle()
                    g_.tensor_tensor(rs2[:, 1, 0:tiles], rs2[:, 0, 0:tiles],
                                     half_pow[0:TILE, 0, 0:tiles], ALU.pow).then_inc(rs_ready, 1)
                st.fill(POOL_STAGE)
                pool.wait_ge(w_ready, r + 1)
                pool.wait_ge(pos_ready, r + 1)
                pool.sem_inc(pool_apart, 1)
                for u in range(tiles):
                    for c in range(2):
                        pool.indirect_dma_start(
                            out=rows_d, out_offset=bass.IndirectOffsetOnAxis(
                                ap=posu[:, u, c:c + 1], axis=0),
                            in_=rows[:, u, :], in_offset=None).then_inc(scattered, 16)

            POOL_START = 32
            me.fill(POOL_START)

            def stage(s):
                if s.routes:
                    route(s, s.g + (-1), 1 - s.parity, TPG)

            each_stage(pool, stage)
            route(None, GROUPS - 1, 0, TILES - FULL_GROUPS * TPG)
            pool.wait_ge(scattered, 32 * TILES + 16)

        @block.scalar
        def _(act):
            a_ = nc.scalar
            b, turn = pro("cols")
            act.wait_ge(pro_ready[b], turn)
            a_.activation(colsT[:, :], gen[b][:, 0:P], ACT.Copy).then_inc(pro_free[b], 1)
            for c in range(5):
                act.wait_ge(ld_x[c], 16 if c < 4 else 32)
                act.wait_ge(rstd_ready, c + 1)
                for t in range(5 * c, 5 * c + 5):
                    ins = a_.activation(xs[:, t, :], xs[:, t, :], ACT.Identity,
                                        bias=rstd[:, 1, t:t + 1], scale=rstd[:, 0, t:t + 1])
                ins.then_inc(xn_ready, 1)
                act.wait_ge(xn_ready, c + 1)
                a_.activation(xn16[:, 0, 5 * c:5 * c + 5, :], xs_chunk(c), ACT.Copy).then_inc(
                    xnh_ready, 1)
            for k in range(SETS):
                for q, tab in (("a", a_tab), ("k", k_tab)):
                    b, turn = pro(f"{q}{k}")
                    act.wait_ge(pro_ready[b], turn)
                    to = tab[:, k * HALVES * TILE:(k + 1) * HALVES * TILE]
                    a_.activation(to.rearrange("p (w h) -> p h w", h=HALVES),
                                  gen[b][:, 0:HALVES * TILE].rearrange("p (h w) -> p h w",
                                                                       h=HALVES),
                                  ACT.Copy).then_inc(pro_free[b], 1)
            act.wait_ge(keys_ready, 1)
            for c in range(5):
                act.wait_ge(head_dev, c + 1)
                if c >= 2:
                    act.wait_ge(head_ss, c - 1)
                a_.activation(squares[c % 2], xs_chunk(c), ACT.Square).then_inc(head_sq, 1)
            act.wait_ge(head_ss, 5)
            a_.activation(head[:, 1, :], head[:, 2, :], ACT.Sqrt,
                          scale=1.0 / (HEADC - 1)).then_inc(head_std, 1)

            def take_counts(g, tiles, fives=ROUNDS // RING, its=None):
                parity = g[1]
                def one(it, r):
                    n = ROUNDS * g[0] + it
                    act.wait_ge(cnt_ready, n + (1 + RING))
                    w = tiles * WIN
                    to = counts[:, parity, :, bass.ds(it * w, w)].rearrange(
                        "p b (u j) -> p b u j", j=WIN)
                    of = ps_cnt[r % 2][:, 0:tiles * KEYS].rearrange(
                        "p (u b j) -> p b u j", u=tiles, j=WIN)
                    a_.activation(to, of, ACT.Copy).then_inc(cnt_taken, 1)
                if its is not None:
                    for it in its:
                        one(it, it % RING)
                    return
                with act.Fori(0, fives) as i:
                    for r in range(RING):
                        one(i * RING + r, r)

            take_counts((0, 0), TPG)
            for c in range(GATES):
                b, turn = pro(f"w{c}")
                act.wait_ge(pro_ready[b], turn)
                a_.activation(w_ih[0][:, :, c * P:(c + 1) * P],
                              gen[b][:, :].rearrange("p (k n) -> p k n", k=HC),
                              ACT.Copy).then_inc(wih_hi, 1)

            def stage(s):
                n = s.n
                for k in range(KC):
                    u = Use(s, f"xnT{k}")
                    act.wait_ge(u.ready, u.turn)
                    a_.activation(xnT[0][:, k, 0:n], u.bank[:, 0:n], ACT.Copy).then_inc(xn_hi, 1)
                if s.build_tiles:
                    take_counts((s.g + 1, 1 - s.parity), s.build_tiles, EARLY)
                act.wait_ge(agg_ready, s.g + 1)
                a_.activation(agg[0][:, 0, 0:n], ps_agg[0][:, 0:n], ACT.Copy)
                a_.activation(agg[0][:, 1, 0:n], ps_agg[1][:, 0:n], ACT.Copy).then_inc(agg_hi, 1)
                for i in range(HC):
                    u = Use(s, f"h{i}")
                    act.wait_ge(u.ready, u.turn)
                    if i >= 2:
                        act.wait_ge(h_lo, s.g * HC + i - 1)
                    a_.activation(h32[:, i % 2, 0:n], u.bank[:, 0:n], ACT.Relu,
                                  bias=colsT[:, C_BREL + i:C_BREL + i + 1]).then_inc(u.free, 1)
                    act.wait_ge(u.free, u.turn)
                    a_.activation(hT[0][:, i, 0:n], h32[:, i % 2, 0:n], ACT.Copy).then_inc(
                        h_hi, 1)

                def gates(j):
                    for q, f in enumerate((ACT.Sigmoid, ACT.Tanh, ACT.Sigmoid)):
                        u = Use(s, f"{'igo'[q]}{j}")
                        act.wait_ge(u.ready, u.turn)
                        a_.activation(gate[:, j % 2, q, 0:n], u.bank[:, 0:n], f,
                                      bias=bg[:, q * HC + j:q * HC + j + 1]).then_inc(u.free, 1)
                        if s.build_tiles:
                            take_counts((s.g + 1, 1 - s.parity), s.build_tiles,
                                        its=LATE[j][q:q + 1 + q // 2])
                    act.wait_ge(c_ready, s.g * HC + j + 1)
                    a_.activation(cell[:, j % 2, 1, 0:n], cell[:, j % 2, 0, 0:n],
                                  ACT.Tanh).then_inc(tc_ready, 1)
                    act.wait_ge(hl_ready, s.g * HC + j + 1)
                    a_.activation(outT[0][:, j, 0:n], out32[:, j % 2, 0:n], ACT.Copy).then_inc(
                        hl_hi, 1)

                gates(0)
                gates(1)
                if s.routes:
                    take_tT(s, TPG)
                gates(2)
                if s.routes:
                    weights(s.g + (-1), TPG)
                gates(3)

            def take_tT(s, tiles):
                u = Use(s, "tT")
                act.wait_ge(u.ready, u.turn)
                a_.activation(tT[:, 0:tiles, :, :].rearrange("p u k n -> p (u k n)"),
                              u.bank[:, 0:tiles * KC * TILE], ACT.Copy).then_inc(u.free, 1)

            def weights(r, tiles):
                act.wait_ge(d_ready, r + 1)
                a_.activation(rows[:, 0:tiles, DIM + 2:DIM + 3], d12[:, 0:tiles, :], ACT.Sigmoid)
                a_.activation(rows[:, 0:tiles, DIM + 3:DIM + 4], d12[:, 0:tiles, :], ACT.Sigmoid,
                              scale=-1.0).then_inc(w_ready, 1)

            each_stage(act, stage)
            end = Stage(GROUPS, 0, 0, TILES - FULL_GROUPS * TPG, 0, True)
            take_tT(end, end.tiles)
            weights(GROUPS - 1, end.tiles)

        @block.tensor
        def _(pe):
            t_ = nc.tensor
            pe.sem_inc(cnt_taken, 2)
            pe.sem_inc(cnt_ready, RING)
            pe.wait_ge(const_ready, 1)
            pe.wait_ge(ld_par, 160)
            b, _ = pro("cols")
            t_.transpose(gen[b][:, 0:P], prow[:, :], ident[:, :]).then_inc(pro_ready[b], 1)
            pe.wait_ge(ok_counted, 1)
            t_.matmul(ps_cnt[0][0:TILE, 0:1], ones[0:TILE, 0:TILE], n_ok[:, :], start=True,
                      stop=True).then_inc(ok_summed, 1)
            pe.wait_ge(keys_ready, 1)
            for k in range(SETS):
                for q, tab in (("a", e_src), ("k", e_dst)):
                    b, turn = pro(f"{q}{k}")
                    if turn > 1:
                        pe.wait_ge(pro_free[b], turn - 1)
                    for h in range(HALVES):
                        ins = t_.transpose(gen[b][:, h * TILE:(h + 1) * TILE],
                                           tab[:, k, h * P:(h + 1) * P].bitcast(F32),
                                           ident[0:TILE, 0:TILE])
                    ins.then_inc(pro_ready[b], 1)

            def build(g, it, r, tiles):
                n = ROUNDS * g + it
                pe.wait_ge(oh_ready, n + 1)
                pe.wait_ge(cnt_taken, n + (2 if r == 0 else 1))
                T = tiles * HALVES
                a = oh_a[:, r, 0:P * T].rearrange("p (a t) -> p a t", t=T)
                k = oh_k[:, r, 0:KEYS * T].rearrange("p (k t) -> p k t", t=T)
                for u in range(tiles):
                    for h in range(HALVES):
                        ins = t_.matmul(ps_cnt[r % 2][:, u * KEYS:(u + 1) * KEYS],
                                        a[:, :, u * HALVES + h], k[:, :, u * HALVES + h],
                                        start=(h == 0), stop=(h == HALVES - 1))
                ins.then_inc(cnt_ready, 1)

            def aggregate(s, it, first, last):
                for k in range(KC):
                    for q in range(2):
                        ins = t_.matmul(ps_agg[k][:, 0:s.n],
                                        xn16[:, q, it, k * P:(k + 1) * P],
                                        counts[:, s.parity, it, 0:s.n],
                                        start=first and q == 0, stop=last and q == 1)
                if last:
                    ins.then_inc(agg_ready, 1)

            def zz(t):
                if t % 5 == 0:
                    pe.wait_ge(z_ready, t // 5 + 1)
                last = t == SRC_BLOCKS - 1
                for k in range(KC):
                    z = xs[:, t, k * P:(k + 1) * P]
                    ins = t_.matmul(ps_zz[k], z, z, start=t == 0 and k == 0,
                                    stop=last and k == KC - 1)

            for i in range(ROUNDS // RING):
                for r in range(RING):
                    build(0, i * RING + r, r, TPG)
                if i in (1, 2):
                    for t in range(5 * (i - 1), 5 * i):
                        zz(t)

            for c in range(GATES):
                j = 3 + c // 2
                pe.wait_ge(ld_raw[j % 2], 16 * (j // 2 + 1))
                b, turn = pro(f"w{c}")
                pe.wait_ge(pro_free[b], turn - 1)
                for k in range(HC):
                    at = (c % 2) * HID + k * P
                    ins = t_.transpose(gen[b][:, k * P:(k + 1) * P], raw[:, j % 2, at:at + P],
                                       ident[:, :])
                ins.then_inc(pro_ready[b], 1)
                if c % 2 == 1:
                    pe.wait_ge(pro_ready[b], turn)
                    pe.sem_inc(raw_used, 1)
                for t in range(10 + 15 * c // GATES, 10 + 15 * (c + 1) // GATES):
                    zz(t)
            pe.wait_ge(zsum_ready, 4)
            for t in range(5):
                ins = t_.matmul(ps_zsum, ones[:, :], zsum[:, t, :], start=(t == 0),
                                stop=(t == 4))
            ins.then_inc(zz_ready, 1)
            for b in range(BANKS):
                pe.wait_ge(pro_free[b], len(PRO[b::BANKS]))
            pe.wait_ge(wlo_ready, 3)
            pe.wait_ge(ld_whi, 48)
            pe.wait_ge(xnl_ready, 5)
            pe.wait_ge(ld_small, 64)
            pe.wait_ge(kv_ready, 1)
            runs_pe = general_runs(pe)
            with pe.If(runs_pe > 0):
                pe.sem_inc(summed, 1)
                pe.sem_inc(sums_ready, SPAN // TILE)
                with pe.Fori(0, SPANS) as i:
                    def column(q, r, start, stop):
                        pe.wait_ge(gathered[r], (i * (COLS // RING) + q) * 16 + 16)
                        pe.wait_ge(oh_dst_ready, i * COLS + q * RING + (r + 1))
                        for j, bank in enumerate(ps_sums):
                            ins = t_.matmul(bank[0:TILE, 0:DIM],
                                            oh_dst[:, j * TILE:(j + 1) * TILE],
                                            src_rows[:, :], start=start, stop=stop)
                        ins.then_inc(summed, 1)

                    pe.wait_ge(sums_ready, (i + 1) * (SPAN // TILE))
                    for r in range(RING):
                        column(0, r, r == 0, False)
                    with pe.Fori(1, COLS // RING - 1) as q:
                        for r in range(RING):
                            column(q, r, False, False)
                    for r in range(RING):
                        column(COLS // RING - 1, r, False, r == RING - 1)
                pe.wait_ge(sums_ready, (SPANS + 1) * (SPAN // TILE))

            def stage(s):
                n, ne = s.n, s.even
                pe.wait_ge(ld_rows[s.parity], (s.pair + 1) * 32)
                for k in range(KC):
                    u = Use(s, f"xnT{k}")
                    if not (isinstance(u.before, int) and u.before == 0):
                        pe.wait_ge(u.free, u.before)
                    for v in range(s.tiles):
                        ins = t_.transpose(u.bank[:, v * TILE:(v + 1) * TILE],
                                           xn_row[:, s.parity, v, k * P:(k + 1) * P],
                                           ident[0:TILE, 0:TILE])
                    ins.then_inc(u.ready, 1)
                pe.wait_ge(cnt_taken, (s.g + 1) * ROUNDS + 2)
                if not (isinstance(s.g, int) and s.g == 0):
                    pe.wait_ge(agg_lo, s.g)

                def five(i, first, last, builds):
                    for r in range(RING):
                        it = i * RING + r
                        if builds:
                            build(s.g + 1, it + (-RING), r, s.build_tiles)
                        aggregate(s, it, first and r == 0, last and r == RING - 1)

                five(0, True, False, 0)
                with pe.If(runs_pe > 0):
                    pe.wait_ge(ld_extra, s.g * 16 + 16)
                    for k in range(KC):
                        for v in range(s.tiles):
                            t_.matmul(ps_agg[k][:, v * TILE:(v + 1) * TILE],
                                      extra[:, v, k * P:(k + 1) * P],
                                      ident[0:TILE, 0:TILE], start=False, stop=False)
                with pe.Fori(1, EARLY + 1) as i:
                    five(i, False, False, s.build_tiles)
                for i in range(EARLY + 1, ROUNDS // RING):
                    five(i, False, i == ROUNDS // RING - 1, 0)

                u = Use(s, "xnT1")
                pe.wait_ge(u.free, u.turn)
                hs = [Use(s, f"h{i}") for i in range(HC)]
                for i, u in enumerate(hs):
                    if not (isinstance(u.before, int) and u.before == 0):
                        pe.wait_ge(u.free, u.before)
                    for k in range(KC):
                        mm3(nc, u.bank[:, 0:ne],
                            (w_root[0][:, k, i * P:(i + 1) * P], w_root[1][:, k, i * P:(i + 1) * P]),
                            (xnT[0][:, k, 0:ne], xnT[1][:, k, 0:ne]), k == 0, False)
                pe.wait_ge(agg_lo, s.g + 1)
                for i, u in enumerate(hs):
                    for k in range(KC):
                        ins = mm3(nc, u.bank[:, 0:ne],
                                  (w_rel[0][:, k, i * P:(i + 1) * P],
                                   w_rel[1][:, k, i * P:(i + 1) * P]),
                                  (agg[0][:, k, 0:ne], agg[1][:, k, 0:ne]), False, k == KC - 1)
                    ins.then_inc(u.ready, 1)

                def gates(j):
                    for q in range(3):
                        u = Use(s, f"{'igo'[q]}{j}")
                        pe.wait_ge(u.free, u.before)
                        c = (q * HC + j) * P
                        for k in range(HC):
                            if j == 0 and q == 0:
                                pe.wait_ge(h_lo, s.g * HC + k + 1)
                            ins = mm3(nc, u.bank[:, 0:ne],
                                      (w_ih[0][:, k, c:c + P], w_ih[1][:, k, c:c + P]),
                                      (hT[0][:, k, 0:ne], hT[1][:, k, 0:ne]), k == 0, k == HC - 1)
                        ins.then_inc(u.ready, 1)
                        if s.build_tiles:
                            for it in LATE[j][q:q + 1 + q // 2]:
                                build(s.g + 1, it, it % RING, s.build_tiles)

                def pass_turn(name):
                    u = Use(s, name)
                    pe.wait_ge(u.free, u.before)
                    pe.sem_inc(u.ready, 1)
                    pe.sem_inc(u.free, 1)

                gates(0)
                gates(1)
                if s.routes:
                    send_tT(s, TPG)
                else:
                    pass_turn("tT")
                gates(2)
                if s.routes:
                    send_logits(s, TPG)
                else:
                    pass_turn("logits")
                gates(3)
                if s.routes:
                    send_rank(s, TPG)
                else:
                    pass_turn("rank")
                for v in range(s.tiles):
                    u = Use(s, f"fc{v}")
                    pe.wait_ge(u.free, u.before)
                    lo, hi = v * TILE, (v + 1) * TILE
                    for k in range(KC):
                        mm3(nc, u.bank[0:TILE, k * P:(k + 1) * P],
                            (xnT[0][:, k, lo:hi], xnT[1][:, k, lo:hi]),
                            (kv[0][:, k, :], kv[1][:, k, :]), k == 0, False)
                    for k in range(HC):
                        if v == 0:
                            pe.wait_ge(hl_lo, s.g * HC + k + 1)
                        ins = mm3(nc, u.bank[0:TILE, 0:DIM],
                                  (outT[0][:, k, lo:hi], outT[1][:, k, lo:hi]),
                                  (w_fc[0][:, k, :], w_fc[1][:, k, :]), False, k == HC - 1)
                    ins.then_inc(u.ready, 1)

            def before(u):
                if not (isinstance(u.before, int) and u.before == 0):
                    pe.wait_ge(u.free, u.before)

            def send_tT(s, tiles):
                r = s.g + (-1)
                u = Use(s, "tT")
                before(u)
                pe.wait_ge(t_ready, r + 1)
                for v in range(tiles):
                    for k in range(KC):
                        at = (v * KC + k) * TILE
                        ins = t_.transpose(u.bank[:, at:at + TILE],
                                           t_row[:, v, k * P:(k + 1) * P],
                                           ident[0:TILE, 0:TILE])
                ins.then_inc(u.ready, 1)

            def send_logits(s, tiles):
                u, of = Use(s, "logits"), Use(s, "tT")
                before(u)
                pe.wait_ge(of.free, of.turn)
                for v in range(tiles):
                    for k in range(KC):
                        ins = t_.matmul(u.bank[0:TILE, v * EXPERTS:(v + 1) * EXPERTS],
                                        tT[:, v, k, :], w_r[:, k, :], start=(k == 0),
                                        stop=(k == KC - 1))
                ins.then_inc(u.ready, 1)

            def send_rank(s, tiles):
                r = s.g + (-1)
                u = Use(s, "rank")
                before(u)
                pe.wait_ge(sel_ready, r + 1)
                E = EXPERTS
                both = [sel[:, 2, v, :] for v in range(tiles)]
                for v in range(tiles):
                    o = u.bank[0:TILE, v * E:(v + 1) * E]
                    t_.matmul(o, tri[:, :], both[v], start=True, stop=(v == 0))
                    if v:
                        t_.matmul(o, ones[0:TILE, 0:TILE], both[0], start=False, stop=True)
                o = u.bank[0:TILE, TPG * E:(TPG + 1) * E]
                for v in range(tiles):
                    ins = t_.matmul(o, ones[0:TILE, 0:TILE], both[v], start=(v == 0),
                                    stop=(v == tiles - 1))
                ins.then_inc(u.ready, 1)

            each_stage(pe, stage)
            end = Stage(GROUPS, 0, 0, TILES - FULL_GROUPS * TPG, 0, True)
            pe.wait_ge(agg_lo, GROUPS)
            send_tT(end, end.tiles)
            send_logits(end, end.tiles)
            send_rank(end, end.tiles)

        @block.vector
        def _(dve):
            v_ = nc.vector
            me = Steps(dve, dve_step)
            DVE_START = 96
            dve.wait_ge(ld_dst, 16)
            v_.tensor_copy(samp[:, :], dst_raw[:, 0:COLS:STRIDE]).then_inc(samp_ready, 1)

            def stats(c):
                dve.wait_ge(ld_x[c], 16 if c < 4 else 32)
                for i in range(5):
                    ins = v_.bn_stats(bn[:, i, :], xs[:, 5 * c + i, :])
                me.did(ins)
                me.settle()
                for i in range(5):
                    ins = v_.bn_aggr(mv[:, 5 * c + i, :], bn[:, i, :])
                ins.then_inc(mv_ready, 1)
                dve.wait_ge(mv_ready, c + 1)

            for c in range(5):
                stats(c)
            dve.wait_ge(const_ready, 1)
            dve.wait_ge(ld_sampb, 16)
            junk = counts[0:TILE, :, :, :].rearrange("p a b c -> p (a b c)")
            for k in range(SETS):
                ins = v_.tensor_scalar(junk[:, 0:SAMPLES] if k % 2 else
                                       junk[:, SAMPLES + 1:2 * SAMPLES + 1], samp_b[0:TILE, :],
                                       thr[:, k:k + 1], 0.0, ALU.is_lt, ALU.add,
                                       accum_out=cnt[:, k:k + 1])
                me.did(ins)
                me.settle()
            c0, c1 = cnt[:, 0:SETS], cnt[:, SETS:2 * SETS]
            me.did(v_.tensor_scalar(c1, c0, -1.0, float(STRIDE), ALU.add, ALU.mult))
            me.settle()
            me.did(v_.tensor_scalar(c0, c1, 0.0, float(EDGES - RUN), ALU.max, ALU.min))
            me.settle()
            v_.tensor_copy(start[:, :], c0).then_inc(start_ready, 1)
            for c in range(5):
                dve.wait_ge(xnh_ready, c + 1)
                v_.tensor_tensor(xn16[:, 1, 5 * c:5 * c + 5, :], xs_chunk(c),
                                 xn16[:, 0, 5 * c:5 * c + 5, :], ALU.subtract).then_inc(
                                     xnl_ready, 1)
            for c in range(5):
                me.did(v_.tensor_reduce(
                    head[:, 2, c * 5 * HEADS:(c + 1) * 5 * HEADS],
                    xs_chunk(c).rearrange("p b (h c) -> p (b h) c", c=HEADC), AX.X, ALU.add))
            me.settle()
            v_.tensor_scalar(head[:, 0, :], head[:, 2, :], 1.0 / HEADC, None,
                             ALU.mult).then_inc(head_sum, 1)
            dve.wait_ge(head_sum, 1)
            dve.wait_ge(ld_edges, 160)
            flat = "p k r -> p (k r)"
            es, ed = e_src[:, :, :].rearrange(flat), e_dst[:, :, :].rearrange(flat)
            esf, edf = es.bitcast(F32), ed.bitcast(F32)
            me.did(v_.tensor_scalar(e_blk, es, 7, None, ALU.logical_shift_right))
            me.settle()
            me.did(v_.tensor_scalar(es, es, P - 1, None, ALU.bitwise_and))
            me.settle()
            me.did(v_.tensor_copy(esf, es))
            me.did(v_.tensor_tensor(e_dst[:, :, :].bitcast(F32), e_dst[:, :, :],
                                    thr[:, :].unsqueeze(2).broadcast_to([TILE, SETS, RUN]),
                                    ALU.subtract))
            me.settle()
            me.did(v_.tensor_scalar(e_ok, edf, 0.0, None, ALU.is_ge))
            me.settle()
            v_.scalar_tensor_tensor(e_ok, edf, float(WIN), e_ok, ALU.is_lt, ALU.mult,
                                    accum_out=n_ok[:, :]).then_inc(ok_counted, 1)
            dve.wait_ge(ok_counted, 1)
            me.did(v_.scalar_tensor_tensor(edf, e_blk, float(WIN), edf, ALU.mult, ALU.add))
            me.settle()
            me.did(v_.scalar_tensor_tensor(edf, edf, 1.0, e_ok, ALU.add, ALU.mult))
            dve.wait_ge(ok_summed, 1)
            me.did(v_.tensor_scalar(covered[:, :], ps_cnt[0][0:TILE, 0:1], float(EDGES), None,
                                    ALU.is_equal))
            me.settle()
            me.did(v_.tensor_scalar(runs_f[:, :], covered[0:1, :], -1.0, 1.0, ALU.mult, ALU.add))
            v_.tensor_scalar(edf, edf, covered[:, 0:1], -1.0, ALU.mult, ALU.add).then_inc(
                keys_ready, 1)
            me.settle()
            v_.tensor_copy(runs[:, :], runs_f[:, :]).then_inc(runs_ready, 1)

            def one_hot(g, it, r, T):
                n = ROUNDS * g + it
                dve.wait_ge(cnt_ready, n + 1)
                at = bass.ds(WPI * HALVES * ROUNDS * g + it * T, T)
                for to, tab, w in ((oh_a, a_tab, P), (oh_k, k_tab, KEYS)):
                    ins = v_.tensor_tensor(
                        to[:, r, 0:w * T].rearrange("p (a t) -> p a t", t=T),
                        iota_rep[:, 0:w, 0:T],
                        tab[:, at].unsqueeze(1).broadcast_to([P, w, T]), ALU.is_equal)
                ins.then_inc(oh_ready, 1)

            def late(s, turn):
                if s.build_tiles:
                    for it in LATE[turn]:
                        one_hot(s.g + 1, it, it % RING, s.build_tiles * HALVES)

            def one_hots(g, tiles, fives=ROUNDS // RING, start=0):
                T = tiles * HALVES
                with dve.Fori(start, fives) as i:
                    for r in range(RING):
                        one_hot(g, i * RING + r, r, T)

            for q in "ak":
                b, turn = pro(f"{q}0")
                dve.wait_ge(pro_free[b], turn)
            for r in range(RING):
                one_hot(0, r, r, TPG * HALVES)
            for c in range(5):
                dve.wait_ge(head_sq, c + 1)
                v_.tensor_reduce(head[:, 2, c * 5 * HEADS:(c + 1) * 5 * HEADS],
                                 squares[c % 2].rearrange("p b (h c) -> p (b h) c", c=HEADC),
                                 AX.X, ALU.add).then_inc(head_ss, 1)
            dve.wait_ge(head_std, 1)
            std, total, inv = head[:, 1, :], head[:, 2, :], head[:, 0, :]
            me.did(v_.tensor_scalar(std, std, 1e-30, None, ALU.max))
            me.settle()
            me.did(v_.reciprocal(inv, std))
            me.settle()
            me.did(v_.scalar_tensor_tensor(inv, total, 1.0 / (HEADC - 1), inv, ALU.mult,
                                           ALU.mult))
            me.settle()
            me.did(v_.tensor_tensor(std, std, inv, ALU.add))
            me.settle()
            me.did(v_.tensor_scalar(std, std, 0.5, 1e-5, ALU.mult, ALU.add))
            me.settle()
            v_.reciprocal(head[:, 2, :], head[:, 1, :]).then_inc(head_inv, 1)

            b, turn = pro("cols")
            dve.wait_ge(pro_free[b], turn)
            me.did(v_.tensor_tensor(bg[:, :], colsT[:, C_BIH:C_BIH + GATES],
                                    colsT[:, C_BHH:C_BHH + GATES], ALU.add))

            for k in range(SETS):
                for q in "ak":
                    b, turn = pro(f"{q}{k}")
                    if k >= SETS - 2:
                        dve.wait_ge(pro_free[b], turn)
            one_hots(0, TPG, start=1)

            for c in range(GATES):
                b, turn = pro(f"w{c}")
                dve.wait_ge(wih_hi, c + 1)
                hi, lo = (w[:, :, c * P:(c + 1) * P] for w in w_ih)
                v_.tensor_tensor(lo, gen[b][:, :].rearrange("p (k n) -> p k n", k=HC), hi,
                                 ALU.subtract).then_inc(pro_free[b], 1)
            dve.wait_ge(ld_small, 64)
            dve.wait_ge(zz_ready, 1)
            wv, bv, S = (t.rearrange("p (k n) -> p k n", k=KC) for t in (
                wv_b[:, :], bv_b[:, :], ps_zsum))
            G = ps_agg[0][:, 0:KC * P].rearrange("p (k n) -> p k n", k=KC)
            t0, t1, t2, t3, t4 = (kvt[:, KC * n:KC * (n + 1), :] for n in range(5))
            diag, heads = (t[:, :].unsqueeze(1).broadcast_to([P, KC, P]) for t in (ident, mask))
            kw, kb = (colsT[:, c:c + KC].unsqueeze(2).broadcast_to([P, KC, P])
                      for c in (C_KW, C_KB))

            def tt(to, a, b, op=ALU.mult):
                me.did(v_.tensor_tensor(to, a, b, op))

            tt(t0, S, diag)
            tt(t1, G, wv)
            tt(t2, S, wv)
            me.settle()
            me.did(v_.tensor_reduce(sd[:, :], t0, AX.X, ALU.add))
            me.settle()
            tt(t3, bv, sd[:, :].unsqueeze(2).broadcast_to([P, KC, P]))
            me.did(v_.scalar_tensor_tensor(t0, bv, float(NODES), t2, ALU.mult, ALU.add))
            me.settle()
            tt(t2, t3, t1, ALU.add)
            tt(t4, t0, kb)
            me.settle()
            tt(t3, t2, kw)
            me.settle()
            tt(t0, t3, t4, ALU.add)
            me.settle()
            tt(t2, t0, heads)
            me.settle()
            tt(t3, t2, diag, ALU.add)
            me.settle()
            me.did(v_.tensor_copy(kv[0][:, :, :], t3))
            me.settle()
            tt(kv[1][:, :, :], t3, kv[0][:, :, :], ALU.subtract)
            me.settle()
            dve.sem_inc(kv_ready, 1)
            me.fill(DVE_START)
            with dve.If(general_runs(dve) > 0):
                dve.wait_ge(span_ready, 1)
                dve.wait_ge(ld_all, 32)
                v_.tensor_copy(dst_f[:, :], all_dst[:, :]).then_inc(dst_step, 1)
                with dve.Fori(0, SPANS) as i:
                    dve.wait_ge(dst_step, i + 1)
                    dve.sem_inc(dve_apart, 1)
                    with dve.Fori(0, COLS) as c:
                        dve.wait_ge(summed, i * COLS + c + 1)
                        v_.tensor_copy(src_at[:, :], all_src[:, bass.ds(c, 1)]).then_inc(
                            src_at_ready, 1)
                        v_.tensor_tensor(oh_dst[:, :], span[:, :],
                                         dst_f[:, bass.ds(c, 1)].broadcast_to([TILE, SPAN]),
                                         ALU.is_equal).then_inc(oh_dst_ready, 1)
                    dve.wait_ge(summed, i * COLS + (COLS + 1))
                    dve.wait_ge(st_sums, i * 16 + 16)
                    for j, bank in enumerate(ps_sums):
                        v_.tensor_copy(sums[:, j, :], bank[0:TILE, 0:DIM]).then_inc(
                            sums_ready, 1)
                    dve.wait_ge(oh_dst_ready, i * COLS + COLS)
                    v_.tensor_scalar(dst_f[:, :], dst_f[:, :], -float(SPAN), None,
                                     ALU.add).then_inc(dst_step, 1)
                dve.wait_ge(dst_step, SPANS + 1)

            def normalise(r, parity, tiles, st):
                def moments(of, turn):
                    for u in range(tiles):
                        ins = v_.bn_stats(bn2[:, u, :], of(u))
                    st.did(ins)
                    st.settle()
                    for u in range(tiles):
                        ins = v_.bn_aggr(mv2[:, u, :], bn2[:, u, :])
                    ins.then_inc(var_ready, 1)
                    dve.wait_ge(var_ready, 2 * r + turn + 1)
                    dve.wait_ge(rs_ready, 2 * r + turn + 1)

                moments(lambda u: x2[:, parity, u, :], 0)
                for u in range(tiles):
                    ins = v_.tensor_scalar(t_row[:, u, :], x2[:, parity, u, :], mv2[:, u, 0:1],
                                           rs2[:, 1, u:u + 1], ALU.subtract, ALU.mult)
                ins.then_inc(t_ready, 1)
                dve.wait_ge(t_ready, r + 1)
                moments(lambda u: t_row[:, u, :], 1)
                dve.wait_ge(scattered, r * (32 * TPG) + 16)
                for u in range(tiles):
                    st.did(v_.tensor_scalar(rows[:, u, 0:DIM], t_row[:, u, :], mv2[:, u, 0:1],
                                            rs2[:, 1, u:u + 1], ALU.subtract, ALU.mult))

            def choose(s, r, tiles, st):
                u = Use(s, "logits")
                dve.wait_ge(u.ready, u.turn)
                T = slice(0, tiles)
                v_.tensor_tensor(lg[:, T, :], u.bank[0:TILE, 0:tiles * EXPERTS].rearrange(
                    "p (u e) -> p u e", e=EXPERTS), br_b[:, :].unsqueeze(1).broadcast_to(
                        [TILE, tiles, EXPERTS]), ALU.add).then_inc(u.free, 1)
                dve.wait_ge(u.free, u.turn)
                dve.sem_inc(dve_apart, 1)
                for v in range(tiles):
                    st.did(v_.max(m8[:, v, :], lg[:, v, :]))
                st.settle()
                for v in range(tiles):
                    st.did(v_.max_index(i8[:, v, :], m8[:, v, :], lg[:, v, :]))
                st.settle()
                st.did(v_.tensor_copy(i8f[:, T, :], i8[:, T, 0:2]))
                v_.tensor_tensor(d12[:, T, :], m8[:, T, 0:1], m8[:, T, 1:2],
                                 ALU.subtract).then_inc(d_ready, 1)
                st.settle()
                io = iota8[:, :].unsqueeze(1).broadcast_to([TILE, tiles, EXPERTS])
                for c in range(2):
                    st.did(v_.tensor_tensor(sel[:, c, T, :], io, i8f[:, T, c:c + 1].broadcast_to(
                        [TILE, tiles, EXPERTS]), ALU.is_equal))
                st.settle()
                v_.tensor_tensor(sel[:, 2, T, :], sel[:, 0, T, :], sel[:, 1, T, :],
                                 ALU.add).then_inc(sel_ready, 1)
                st.did(v_.tensor_copy(rows[:, T, DIM:DIM + 1],
                                      ids[:, bass.ds(r * TPG, tiles)].unsqueeze(2)))
                st.did(v_.tensor_copy(rows[:, T, DIM + 1:DIM + 2], i8f[:, T, 0:1]))

            def place(s, r, tiles, st):
                u = Use(s, "rank")
                T, E = slice(0, tiles), EXPERTS
                dve.wait_ge(u.ready, u.turn)
                st.did(v_.tensor_tensor(pos[:, T, :], u.bank[0:TILE, 0:tiles * E].rearrange(
                    "p (u e) -> p u e", e=E), carry[:, :].unsqueeze(1).broadcast_to(
                        [TILE, tiles, E]), ALU.add))
                st.settle()
                v_.tensor_tensor(carry[:, :], carry[:, :],
                                 u.bank[0:TILE, TPG * E:(TPG + 1) * E], ALU.add).then_inc(
                                     u.free, 1)
                dve.wait_ge(u.free, u.turn)
                st.settle()
                for c in range(2):
                    st.did(v_.tensor_tensor(posx[:, c, T, :], pos[:, T, :], sel[:, c, T, :],
                                            ALU.mult))
                st.settle()
                for c in range(2):
                    st.did(v_.tensor_reduce(posf[:, T, c], posx[:, c, T, :], AX.X, ALU.add))
                st.settle()
                v_.tensor_copy(posu[:, T, :], posf[:, T, :]).then_inc(pos_ready, 1)

            def stage(s):
                st = Steps(dve, dve_step, s.g * DVE_STAGE + DVE_START, dve_apart)
                n, r = s.n, s.g + (-1)
                for k in range(KC):
                    u = Use(s, f"xnT{k}")
                    dve.wait_ge(xn_hi, s.g * KC + k + 1)
                    v_.tensor_tensor(xnT[1][:, k, 0:n], u.bank[:, 0:n], xnT[0][:, k, 0:n],
                                     ALU.subtract).then_inc(u.free, 1)
                if s.build_tiles:
                    one_hots(s.g + 1, s.build_tiles, EARLY)
                if s.routes:
                    normalise(r, 1 - s.parity, TPG, st)
                late(s, 0)
                dve.wait_ge(agg_hi, s.g + 1)
                for k in range(KC):
                    ins = v_.tensor_tensor(agg[1][:, k, 0:n], ps_agg[k][:, 0:n],
                                           agg[0][:, k, 0:n], ALU.subtract)
                ins.then_inc(agg_lo, 1)
                for i in range(HC):
                    dve.wait_ge(h_hi, s.g * HC + i + 1)
                    v_.tensor_tensor(hT[1][:, i, 0:n], h32[:, i % 2, 0:n], hT[0][:, i, 0:n],
                                     ALU.subtract).then_inc(h_lo, 1)

                def cell_out(j):
                    if j < HC - 1:
                        late(s, j + 1)
                    ui, ug, uo = (Use(s, f"{q}{j}") for q in "igo")
                    at = s.g * HC + j + 1
                    dve.wait_ge(ui.free, ui.turn)
                    dve.wait_ge(ug.free, ug.turn)
                    v_.tensor_tensor(cell[:, j % 2, 0, 0:n], gate[:, j % 2, 0, 0:n],
                                     gate[:, j % 2, 1, 0:n], ALU.mult).then_inc(c_ready, 1)
                    dve.wait_ge(tc_ready, at)
                    dve.wait_ge(uo.free, uo.turn)
                    v_.tensor_tensor(out32[:, j % 2, 0:n], gate[:, j % 2, 2, 0:n],
                                     cell[:, j % 2, 1, 0:n], ALU.mult).then_inc(hl_ready, 1)
                    dve.wait_ge(hl_hi, at)
                    v_.tensor_tensor(outT[1][:, j, 0:n], out32[:, j % 2, 0:n],
                                     outT[0][:, j, 0:n], ALU.subtract).then_inc(hl_lo, 1)

                cell_out(0)
                cell_out(1)
                cell_out(2)
                if s.routes:
                    choose(s, r, TPG, st)
                cell_out(3)
                if s.routes:
                    place(s, r, TPG, st)
                dve.wait_ge(ld_rows[s.parity], (s.pair + 1) * 32)
                dve.wait_ge(st_x2[s.parity], s.pair * 16 + 16)
                st.did(v_.tensor_tensor(
                    x2[:, s.parity, 0:s.tiles, :], x_row[:, s.parity, 0:s.tiles, :],
                    bfc_b[:, :].unsqueeze(1).broadcast_to([TILE, s.tiles, DIM]), ALU.add))
                st.settle()
                for v in range(s.tiles):
                    u = Use(s, f"fc{v}")
                    dve.wait_ge(u.ready, u.turn)
                    o = x2[:, s.parity, v, :]
                    v_.tensor_tensor(o, o, u.bank[0:TILE, 0:DIM], ALU.add).then_inc(u.free, 1)
                    dve.wait_ge(u.free, u.turn)
                dve.sem_inc(x2_ready, 1)
                st.fill(DVE_STAGE)

            each_stage(dve, stage)
            st = Steps(dve, dve_step, GROUPS * DVE_STAGE + DVE_START)
            end = Stage(GROUPS, 0, 0, TILES - FULL_GROUPS * TPG, 0, True)
            normalise(GROUPS - 1, 0, end.tiles, st)
            choose(end, GROUPS - 1, end.tiles, st)
            place(end, GROUPS - 1, end.tiles, st)


def moe_phase(nc, sem, keep, rows_d, acc_d, W1, W2, b2, out):
    ident, colsT, carry = keep.ident, keep.colsT, keep.carry
    ps_l1, ps_y, ps_x = keep.banks[0:4], keep.banks[4:6], keep.banks[6]
    SUB = SLOTS // P
    LIST = MAXBLK + NODES // SLOTS + 2
    K_BLK, K_BASE, K_END, K_EXP = 0, EXPERTS, 2 * EXPERTS + 1, 3 * EXPERTS + 1
    LAG = 3
    MORE = NODES // SLOTS

    with ExitStack() as ctx:
        m_ = Memory(nc, ctx)
        raw = m_.sbuf("raw_e", [P, 2, 4, RAW], F32)
        w1 = [m_.sbuf(f"w1{q}", [P, 2, KC, FF], F32R) for q in "hl"]
        w2 = [m_.sbuf(f"w2{q}", [P, 2, MC, DIM], F32R) for q in "hl"]
        b2_b = m_.sbuf("b2_b", [P, EXPERTS * DIM], F32)
        x_blk = m_.sbuf("x_blk", [P, SUB, ROW], F32)
        xT32 = m_.sbuf("xT32", [P, KC, SLOTS], F32)
        xT = [m_.sbuf(f"xT{q}", [P, KC, SLOTS], F32R) for q in "hl"]
        g32 = m_.sbuf("g32", [P, 2, SLOTS], F32)
        gT = [m_.sbuf(f"gT{q}", [P, MC, SLOTS], F32R) for q in "hl"]
        y_raw = m_.sbuf("y_raw", [P, SUB, DIM], F32)
        y = m_.sbuf("y", [P, SUB, DIM], F32)
        meta = m_.sbuf("meta", [P, SUB, 4], F32)
        first = m_.sbuf("first", [P, SUB], F32)
        part = m_.sbuf("part", [P, 2, SUB], F32)
        wsel = m_.sbuf("wsel", [P, SUB], F32)
        uid = m_.sbuf("uid", [P, SUB], U32)
        e_col = m_.sbuf("e_col", [P, EXPERTS], F32)
        pad = m_.sbuf("pad", [P, SUB, ROW], F32)
        ecap = m_.sbuf("ecap", [1, EXPERTS], F32)
        steps = m_.sbuf("steps", [1, MORE], F32)
        numbers = m_.sbuf("numbers", [1, LIST], F32)
        tabf = m_.sbuf("tabf", [1, K_EXP + LIST], F32)
        tabi = m_.sbuf("tabi", [1, K_EXP + LIST], I32)
        spare = m_.sbuf("spare", [1, 1], F32)
        over = m_.sbuf("over", [1, EXPERTS, MORE], F32)
        past = m_.sbuf("past", [1, LIST, EXPERTS], F32)

        moe_const, tab_ready, st_pad0, st_pad, ld_b2, ld_blk = (
            sem(n) for n in ("moe_const", "moe_tab", "st_pad0", "st_pad", "ld_b2", "ld_blk"))
        ld_raw_e = [sem(f"ld_raw_e{p}") for p in range(2)]
        w_hi0, w_hi, w_lo = sem("w_hi0"), sem("w_hi"), sem("w_lo")
        xt_ready, xt_free, meta_taken, xh_ready, xl_ready = (
            sem(n) for n in ("xt_ready", "xt_free", "meta_taken", "xh_ready", "xl_ready"))
        l1_ready = [sem(f"l1_ready{b}") for b in range(4)]
        l1_free = [sem(f"l1_free{b}") for b in range(4)]
        gh_ready, gl_ready, l2_done, y_free, y_ready, added = (
            sem(n) for n in ("gh_ready", "gl_ready", "l2_done", "y_free", "y_ready", "added"))
        mdve, mpool, mapart, mpapart, st_out = (
            sem(n) for n in ("mdve", "mpool", "mapart", "mpapart", "st_out"))
        block = ctx.enter_context(nc.Block())

        def first_weights(j):
            if j < 2:
                return tuple(w[:, 0, j, :] for w in w1)
            return tuple(w[:, 0, 4 * (j - 2):4 * (j - 1), :].rearrange("p m n -> p (m n)")
                         for w in w2)

        def wait_some(eng, of, count):
            if not (isinstance(count, int) and count == 0):
                eng.wait_ge(of, count)

        def look(eng, at, lo, hi):
            return eng.value_load(tabi[0:1, at:at + 1], min_val=lo, max_val=hi)

        def experts(eng, body):
            def two(pair):
                for parity in range(2):
                    e = pair * 2 + parity
                    count = eng.value_load(tabi[0:1, bass.ds(e + K_BLK, 1)], min_val=1,
                                           max_val=MORE + 1)
                    base = eng.value_load(tabi[0:1, bass.ds(e + K_BASE, 1)], min_val=0,
                                          max_val=MAXBLK - 1)
                    body(e, pair, parity, base, count)

            eng.wait_ge(tab_ready, 1)
            with eng.Fori(0, EXPERTS // 2 - 1) as pair:
                two(pair)
            two(EXPERTS // 2 - 1)

        @block.sync
        def _(sp):
            def load_raw(e, parity):
                for j in range(4):
                    if j < 2:
                        of = W1[bass.ds(e, 1), j * P:(j + 1) * P, :].rearrange("e p n -> p (e n)")
                        to = raw[:, parity, j, :]
                    else:
                        r = (j - 2) * 4 * P
                        of = W2[bass.ds(e, 1), r:r + 4 * P, :].rearrange(
                            "e (m p) n -> p (e m) n", p=P)
                        to = raw[:, parity, j, :].rearrange("p (m n) -> p m n", m=4)
                    sp.dma_start(to, of).then_inc(ld_raw_e[parity], 16)

            load_raw(0, 0)
            sp.wait_ge(tab_ready, 1)
            sp.wait_ge(moe_const, 1)
            def fill(e, stored):
                end = look(sp, K_END + e, e * CAP, e * CAP + NODES)
                sp.dma_start(rows_d[bass.ds(end, SLOTS), :].rearrange("(h p) f -> p h f", p=P),
                             pad[:, :, :]).then_inc(stored, 16)

            fill(0, st_pad0)
            sp.wait_ge(st_pad0, 16)

            def load_block(row, n):
                wait_some(sp, xt_ready, n)
                wait_some(sp, meta_taken, n)
                sp.dma_start(x_blk[:, :, :], rows_d[bass.ds(row, SLOTS), :].rearrange(
                    "(h p) f -> p h f", p=P)).then_inc(ld_blk, 16)

            load_block(0, 0)
            for e in range(1, EXPERTS):
                fill(e, st_pad)
            sp.dma_start(b2_b[:, :], b2.rearrange("e n -> (e n)").unsqueeze(0).broadcast_to(
                [P, EXPERTS * DIM])).then_inc(ld_b2, 16)
            sp.wait_ge(st_pad, 16 * (EXPERTS - 1))

            def expert(e, pair, parity, base, count):
                with sp.If(count > 1):
                    load_block(e * CAP + SLOTS, base + 1)
                if parity == 0:
                    sp.wait_ge(w_lo, pair * 8 + 4)
                    load_raw(e + 1, 1)
                else:
                    if not isinstance(e, int):
                        sp.wait_ge(w_lo, pair * 8 + 4)
                        load_raw(e + 1, 0)
                with sp.If(count > 2):
                    with sp.Fori(2, count) as i:
                        load_block(e * CAP + i * SLOTS, base + i)
                load_block((e + 1) * CAP if not (isinstance(e, int) and e == EXPERTS - 1) else 0,
                           base + count)

            experts(sp, expert)
            total = look(sp, K_BASE + EXPERTS, EXPERTS, MAXBLK)
            sp.wait_ge(added, total * (16 * SUB) + 16)
            sp.dma_start(out, acc_d[0:NODES, :]).then_inc(st_out, 16)
            sp.wait_ge(st_out, 16)

        @block.gpsimd
        def _(pool):
            g_ = nc.gpsimd
            me = Steps(pool, mpool)
            g_.iota(ecap[:, :], pattern=[[CAP, EXPERTS]], base=0, channel_multiplier=0,
                    allow_small_or_imprecise_dtypes=True)
            g_.iota(e_col[:, :], pattern=[[1, EXPERTS]], base=0, channel_multiplier=0,
                    allow_small_or_imprecise_dtypes=True)
            g_.iota(steps[:, :], pattern=[[SLOTS, MORE]], base=SLOTS, channel_multiplier=0,
                    allow_small_or_imprecise_dtypes=True)
            g_.iota(numbers[:, :], pattern=[[1, LIST]], base=0, channel_multiplier=0,
                    allow_small_or_imprecise_dtypes=True)
            me.did(g_.memset(pad[:, :, :], 0.0))
            me.settle()
            g_.iota(pad[:, :, DIM:DIM + 1], pattern=[[P, SUB], [0, 1]], base=NODES,
                    channel_multiplier=1,
                    allow_small_or_imprecise_dtypes=True).then_inc(moe_const, 1)
            pool.wait_ge(moe_const, 1)
            pool.dma_start(acc_d[NODES:NODES + SLOTS, :].rearrange("(h p) f -> p h f", p=P),
                           pad[:, :, 0:DIM]).then_inc(added, 16)

            def load_hi(e, parity):
                pool.dma_start(w1[0][:, parity, :, :], W1[bass.ds(e, 1), :, :].rearrange(
                    "e (k p) n -> p (e k) n", p=P)).then_inc(w_hi, 16)
                pool.dma_start(w2[0][:, parity, :, :], W2[bass.ds(e, 1), :, :].rearrange(
                    "e (m p) n -> p (e m) n", p=P)).then_inc(w_hi, 16)

            def split(e, pair, parity):
                pool.wait_ge(w_hi, e * 32)
                pool.wait_ge(ld_raw_e[parity], (pair + 1) * 64)
                for j in range(4):
                    if j < 2:
                        hi, lo = (w[:, parity, j, :] for w in w1)
                    else:
                        hi, lo = (w[:, parity, 4 * (j - 2):4 * (j - 1), :].rearrange(
                            "p m n -> p (m n)") for w in w2)
                    g_.tensor_tensor(lo, raw[:, parity, j, :], hi, ALU.subtract).then_inc(w_lo, 1)

            pool.wait_ge(w_lo, 4)

            def add_block(n):
                for h in range(SUB):
                    at = n * SUB + h
                    pool.wait_ge(y_ready, at + 1)
                    pool.wait_ge(added, at * 16 + 16)
                    pool.sem_inc(mpapart, 1)
                    pool.indirect_dma_start(
                        out=acc_d, out_offset=bass.IndirectOffsetOnAxis(ap=uid[:, h:h + 1],
                                                                        axis=0),
                        in_=y[:, h, :], in_offset=None, compute_op=ALU.add).then_inc(added, 16)

            def expert(e, pair, parity, base, count):
                more = parity == 0 or not isinstance(e, int)
                if more:
                    pool.wait_ge(ld_blk, base * 16 + 32)
                    pool.sem_inc(mpapart, 1)
                    load_hi(e + 1, 1 - parity)
                add_block(base)
                if more:
                    split(e + 1, pair + parity, 1 - parity)
                with pool.If(count > 1):
                    with pool.Fori(1, count) as i:
                        add_block(base + i)

            experts(pool, expert)

        @block.scalar
        def _(act):
            a_ = nc.scalar

            def take_x(n):
                e = act.value_load(tabi[0:1, bass.ds(n + K_EXP, 1)], min_val=0,
                                   max_val=EXPERTS - 1)
                act.wait_ge(xt_ready, n + 1)
                wait_some(act, xl_ready, n * KC)
                for k in range(KC):
                    ins = a_.activation(xT32[:, k, :], ps_x[:, k * SLOTS:(k + 1) * SLOTS],
                                        ACT.Identity,
                                        bias=colsT[:, bass.ds(e * KC + (C_LNB + k), 1)],
                                        scale=colsT[:, bass.ds(e * KC + (C_LNG + k), 1)])
                ins.then_inc(xt_free, 1)

            def split_x(n):
                act.wait_ge(xt_free, n + 1)
                wait_some(act, l1_ready[3], n * 2)
                for k in range(KC):
                    a_.activation(xT[0][:, k, :], xT32[:, k, :], ACT.Copy).then_inc(xh_ready, 1)

            a_.activation(spare[:, :], ident[0:1, 0:1], ACT.Gelu)
            act.wait_ge(ld_raw_e[0], 64)
            for j in range(4):
                if j == 2:
                    act.wait_ge(tab_ready, 1)
                    take_x(0)
                    split_x(0)
                a_.activation(first_weights(j)[0], raw[:, 0, j, :], ACT.Copy).then_inc(w_hi0, 1)

            def expert(e, pair, parity, base, count):
                with act.Fori(0, count) as i:
                    n = base + i
                    for m in range(MC):
                        b = m % 4
                        act.wait_ge(l1_ready[b], n * 2 + (m // 4 + 1))
                        act.wait_ge(gl_ready, n * MC + (m + 1))
                        a_.activation(g32[:, m % 2, :], ps_l1[b][:, 0:SLOTS], ACT.Gelu,
                                      bias=colsT[:, bass.ds(e * MC + (C_B1 + m), 1)]).then_inc(
                                          l1_free[b], 1)
                        act.wait_ge(l1_free[b], n * 2 + (m // 4 + 2))
                        act.wait_ge(l2_done, n * MC + (m + 1))
                        a_.activation(gT[0][:, m, :], g32[:, m % 2, :], ACT.Copy).then_inc(
                            gh_ready, 1)
                        if m == 5:
                            take_x(n + 1)
                    split_x(n + 1)

            experts(act, expert)

        @block.tensor
        def _(pe):
            t_ = nc.tensor
            pe.sem_inc(gl_ready, 2)
            pe.sem_inc(l2_done, MC)
            for b in range(4):
                pe.sem_inc(l1_free[b], 1)
            pe.sem_inc(y_free, 1)

            def transpose_x(n):
                pe.wait_ge(ld_blk, n * 16 + 16)
                wait_some(pe, xt_free, n)
                for h in range(SUB):
                    for k in range(KC):
                        at = k * SLOTS + h * P
                        ins = t_.transpose(ps_x[:, at:at + P], x_blk[:, h, k * P:(k + 1) * P],
                                           ident[:, :])
                ins.then_inc(xt_ready, 1)

            transpose_x(0)

            def expert(e, pair, parity, base, count):
                pe.wait_ge(w_lo, e * 4 + 2)
                pe.sem_inc(mapart, 1)
                with pe.Fori(0, count) as i:
                    n = base + i

                    def layer1(m):
                        b = m % 4
                        pe.wait_ge(l1_free[b], n * 2 + (m // 4 + 1))
                        c = slice(m * P, (m + 1) * P)
                        for k in range(KC):
                            if m == 0:
                                pe.wait_ge(xl_ready, n * KC + (k + 1))
                            ins = mm3(nc, ps_l1[b][:, 0:SLOTS],
                                      tuple(w[:, parity, k, c] for w in w1),
                                      tuple(x[:, k, :] for x in xT), k == 0, k == KC - 1)
                        ins.then_inc(l1_ready[b], 1)

                    def layer2(m):
                        if m == 0:
                            pe.wait_ge(y_free, n + 1)
                            pe.wait_ge(w_lo, (e + 1) * 4)
                        pe.wait_ge(gl_ready, n * MC + (m + 3))
                        for h in range(SUB):
                            ins = mm3(nc, ps_y[h][:, 0:DIM],
                                      tuple(g[:, m, h * P:(h + 1) * P] for g in gT),
                                      tuple(w[:, parity, m, :] for w in w2), m == 0,
                                      m == MC - 1)
                        ins.then_inc(l2_done, 1)

                    for m in range(MC):
                        layer1(m)
                        if m >= LAG:
                            layer2(m - LAG)
                        if m == 5:
                            transpose_x(n + 1)
                    for m in range(MC - LAG, MC):
                        layer2(m)

            experts(pe, expert)

        @block.vector
        def _(dve):
            v_ = nc.vector
            me = Steps(dve, mdve)
            dve.wait_ge(moe_const, 1)
            E = EXPERTS
            blk, base_, end_ = (tabf[:, a:a + n] for a, n in (
                (K_BLK, E), (K_BASE, E + 1), (K_END, E)))
            exp = tabf[:, K_EXP:K_EXP + LIST]
            me.did(v_.tensor_copy(end_, carry[0:1, :]))
            me.did(v_.memset(base_[:, 0:1], 0.0))
            me.did(v_.tensor_tensor(ecap[:, :], carry[0:1, :], ecap[:, :], ALU.subtract))
            me.settle()
            me.did(v_.tensor_tensor(over[:, :, :], ecap[:, :].unsqueeze(2).broadcast_to(
                [1, E, MORE]), steps[:, :].unsqueeze(1).broadcast_to([1, E, MORE]), ALU.is_gt))
            me.settle()
            me.did(v_.tensor_reduce(blk, over[:, :, :], AX.X, ALU.add))
            me.settle()
            me.did(v_.tensor_scalar(blk, blk, 1.0, None, ALU.add))
            me.settle()
            for e in range(E):
                me.did(v_.tensor_tensor(base_[:, e + 1:e + 2], base_[:, e:e + 1],
                                        blk[:, e:e + 1], ALU.add))
                me.settle()
            me.did(v_.tensor_tensor(past[:, :, :], numbers[:, :].unsqueeze(2).broadcast_to(
                [1, LIST, E]), base_[:, 0:E].unsqueeze(1).broadcast_to([1, LIST, E]), ALU.is_ge))
            me.settle()
            me.did(v_.tensor_reduce(exp, past[:, :, :], AX.X, ALU.add))
            me.settle()
            me.did(v_.tensor_scalar(exp, exp, -1.0, None, ALU.add))
            me.settle()
            v_.tensor_copy(tabi[:, :], tabf[:, :]).then_inc(tab_ready, 1)

            OUT_STEPS = 8
            START = 40
            me.fill(START)

            def split_x(n):
                for k in range(KC):
                    dve.wait_ge(xh_ready, n * KC + (k + 1))
                    v_.tensor_tensor(xT[1][:, k, :], xT32[:, k, :], xT[0][:, k, :],
                                     ALU.subtract).then_inc(xl_ready, 1)

            def take_meta(n):
                dve.wait_ge(ld_blk, n * 16 + 16)
                v_.tensor_copy(meta[:, :, :], x_blk[:, :, DIM:ROW]).then_inc(meta_taken, 1)

            take_meta(0)
            dve.wait_ge(ld_raw_e[0], 64)
            for j in range(4):
                if j == 2:
                    split_x(0)
                dve.wait_ge(w_hi0, j + 1)
                hi, lo = first_weights(j)
                v_.tensor_tensor(lo, raw[:, 0, j, :], hi, ALU.subtract).then_inc(w_lo, 1)
            dve.wait_ge(ld_b2, 16)

            def expert(e, pair, parity, base, count):
                with dve.Fori(0, count) as i:
                    n = base + i
                    st = Steps(dve, mdve, n * OUT_STEPS + START)
                    for m in range(MC):
                        dve.wait_ge(gh_ready, n * MC + (m + 1))
                        v_.tensor_tensor(gT[1][:, m, :], g32[:, m % 2, :], gT[0][:, m, :],
                                         ALU.subtract).then_inc(gl_ready, 1)
                        if m != MC // 2:
                            continue
                        dve.wait_ge(meta_taken, n + 1)
                        st.did(v_.tensor_tensor(first[:, :], meta[:, :, 1],
                                                e_col[:, bass.ds(e, 1)].broadcast_to([P, SUB]),
                                                ALU.is_equal))
                        st.settle()
                        st.did(v_.tensor_tensor(part[:, 0, :], meta[:, :, 2], first[:, :], ALU.mult))
                        st.did(v_.scalar_tensor_tensor(part[:, 1, :], first[:, :], -1.0,
                                                       meta[:, :, 3], ALU.add, ALU.mult))
                        st.settle()
                        st.did(v_.tensor_tensor(wsel[:, :], part[:, 0, :], part[:, 1, :],
                                                ALU.subtract))
                    split_x(n + 1)
                    dve.wait_ge(l2_done, n * MC + 2 * MC)
                    for h in range(SUB):
                        ins = v_.tensor_tensor(y_raw[:, h, :], ps_y[h][:, 0:DIM],
                                               b2_b[:, bass.ds(e * DIM, DIM)], ALU.add)
                        if h == 0:
                            st.did(ins)
                        else:
                            ins.then_inc(y_free, 1)
                    dve.wait_ge(added, n * (16 * SUB) + 16)
                    st.did(v_.tensor_copy(uid[:, :], meta[:, :, 0]))
                    st.settle()
                    dve.wait_ge(y_free, n + 2)
                    for h in range(SUB):
                        v_.tensor_scalar(y[:, h, :], y_raw[:, h, :], wsel[:, h:h + 1], None,
                                         ALU.mult).then_inc(y_ready, 1)
                    take_meta(n + 1)
                    st.fill(OUT_STEPS)

            experts(dve, expert)


_INS = ["x", "src", "dst", "L0_gnn_W_rel", "L0_gnn_b_rel", "L0_gnn_W_root", "L0_gnn_W_ih",
        "L0_gnn_W_hh", "L0_gnn_b_ih", "L0_gnn_b_hh", "L0_gnn_W_fc", "L0_gnn_b_fc",
        "L0_mix_kln_weight", "L0_mix_kln_bias", "L0_mix_vln_weight", "L0_mix_vln_bias",
        "L0_ffn_Wr", "L0_ffn_br", "L0_ffn_ln_g", "L0_ffn_ln_b", "L0_ffn_W1", "L0_ffn_b1",
        "L0_ffn_W2", "L0_ffn_b2"]


def kernel(**inputs):
    import concourse.bacc as _bacc
    from concourse.bass_utils import run_bass_kernel_spmd as _run

    nc = _bacc.Bacc("TRN2", target_bir_lowering=False, num_devices=1)
    arrays, args = {}, []
    for name in _INS:
        a = np.ascontiguousarray(inputs[name])
        arrays[f"in_{name}"] = a
        args.append(nc.dram_tensor(f"in_{name}", a.shape, mybir.dt.from_np(a.dtype),
                                   kind="ExternalInput").ap())
    args.append(nc.dram_tensor("out_0", (NODES, DIM), F32, kind="ExternalOutput").ap())
    program(nc, *args)
    r = _run(nc, [arrays], core_ids=[0])
    return r.results[0]["out_0"]
```
